# Optimizing a Trainium2 kernel written in Bass

```python
import numpy as np
import jax
import jax.numpy as jnp

def _softmax(x, axis=-1):
    return jax.nn.softmax(x, axis=axis)

def _gelu(x):
    return jax.nn.gelu(x, approximate=True)

def _silu(x):
    return jax.nn.silu(x)

def _sigmoid(x):
    return jax.nn.sigmoid(x)

def _layernorm(x, axis=-1, eps=1e-05):
    m = jnp.mean(x, axis=axis, keepdims=True)
    v = jnp.var(x, axis=axis, keepdims=True)
    return (x - m) / jnp.sqrt(v + eps)

def _scatter_add(tgt, idx, src, axis=0):
    return tgt.at[idx].add(src)

def _segment_sum(src, seg, n):
    return jax.ops.segment_sum(src, seg, n)
kernel_name = 'mk_xattn_ffn_d1_seqx_r8_d7d099'

def setup_inputs(seed: int=0):
    np.random.seed(seed)
    _w = jnp.asarray

    def _rec_inputs():
        import jax
        import jax.numpy as jnp
        _rk = jax.random.key(seed)
        x = 7.22e-05 + 1 * jax.random.normal(jax.random.fold_in(_rk, 1), (64, 64, 256), jnp.float32)
        _lenS = 64 - jax.random.randint(jax.random.fold_in(_rk, 7), (64,), 0, max(1, 64 // 4) + 1, jnp.int32)
        _lenS2 = 64 - jax.random.randint(jax.random.fold_in(_rk, 8), (64,), 0, max(1, 64 // 4) + 1, jnp.int32)
        _ctx_512P = jax.random.normal(jax.random.fold_in(_rk, 11), (64, 16, 64), jnp.float32)
        _ctx_512c = jax.random.dirichlet(jax.random.fold_in(_rk, 511), 0.3 * jnp.ones((16,), jnp.float32), (64, 64))
        _ctx_512t = jnp.einsum('bsk,bkd->bsd', _ctx_512c, _ctx_512P)
        _ctx_512t = _ctx_512t * jax.lax.rsqrt(jnp.mean(jnp.square(_ctx_512t)) + 1e-12) * 0.953939
        ctx_512 = -0.000514642 + 1.00011 * (_ctx_512t + 0.3 * jax.random.normal(jax.random.fold_in(_rk, 611), (64, 64, 64), jnp.float32))
        return (x, ctx_512)
    x, ctx_512 = _rec_inputs()

    def _L0_xattn_setup():
        import jax, jax.numpy as jnp
        import numpy as np
        B, S, E = (2, 256, 256)
        QH, KVH = (32, 8)
        D = E // QH
        G = QH // KVH
        DROPOUT = 1.0
        key = jax.random.key(seed)
        k1, k2, k3 = jax.random.split(key, 3)
        q = jax.random.normal(k1, (B, S, E), dtype=jnp.float32)
        k = jax.random.normal(k2, (B, S, E // G), dtype=jnp.float32)
        v = jax.random.normal(k3, (B, S, E // G), dtype=jnp.float32)
        return {'q': q, 'k': k, 'v': v}
    _L0_xattn_all = _L0_xattn_setup()
    _L0_xattn_in = {k: v for k, v in _L0_xattn_all.items() if k in ()}
    del _L0_xattn_all

    def _L0_ffn_setup():
        import jax, jax.numpy as jnp
        import numpy as np
        HIDDEN = 256
        INTER = 96
        N_EXPERTS = 32
        TOP_K = 8
        key = jax.random.key(seed)
        k = jax.random.split(key, 5)
        s = 1.0 / np.sqrt(HIDDEN)
        return {'hidden_states': jax.random.normal(k[0], (1, 128, HIDDEN), jnp.float32), 'gate_w': jax.random.normal(k[1], (HIDDEN, N_EXPERTS), jnp.float32) * s, 'w_gate': jax.random.normal(k[2], (N_EXPERTS, HIDDEN, INTER), jnp.float32) * s, 'w_up': jax.random.normal(k[3], (N_EXPERTS, HIDDEN, INTER), jnp.float32) * s, 'w_down': jax.random.normal(k[4], (N_EXPERTS, INTER, HIDDEN), jnp.float32) * (1.0 / np.sqrt(INTER))}
    _L0_ffn_all = _L0_ffn_setup()
    _L0_ffn_in = {k: v for k, v in _L0_ffn_all.items() if k in ('gate_w', 'w_gate', 'w_up', 'w_down')}
    del _L0_ffn_all
    return {'x': x, 'ctx_512': ctx_512, 'L0_ffn_gate_w': _L0_ffn_in['gate_w'], 'L0_ffn_w_gate': _L0_ffn_in['w_gate'], 'L0_ffn_w_up': _L0_ffn_in['w_up'], 'L0_ffn_w_down': _L0_ffn_in['w_down']}

def reference(x, ctx_512, L0_ffn_gate_w, L0_ffn_w_gate, L0_ffn_w_up, L0_ffn_w_down):
    import jax
    import jax.numpy as jnp

    def _L0_xattn_ref(q, k, v):
        import jax, jax.numpy as jnp
        import numpy as np
        B, S, E = (2, 256, 256)
        QH, KVH = (32, 8)
        D = E // QH
        G = QH // KVH
        DROPOUT = 1.0
        b, s, _ = q.shape
        qh = q.reshape(b, s, KVH, G, D).transpose(0, 2, 3, 1, 4)
        kh = k.reshape(b, s, KVH, D).transpose(0, 2, 1, 3)
        vh = v.reshape(b, s, KVH, D).transpose(0, 2, 1, 3)
        scale = 1.0 / jnp.sqrt(jnp.float32(D))
        scores = jnp.einsum('bkgsd,bktd->bkgst', qh, kh) * scale
        attn = jax.nn.softmax(scores, axis=-1) / DROPOUT
        out = jnp.einsum('bkgst,bktd->bkgsd', attn, vh)
        return out.transpose(0, 3, 1, 2, 4).reshape(b, s, E)

    def _L0_ffn_ref(hidden_states, gate_w, w_gate, w_up, w_down):
        import jax, jax.numpy as jnp
        import numpy as np
        HIDDEN = 256
        INTER = 96
        N_EXPERTS = 32
        TOP_K = 8
        B, S, H = hidden_states.shape
        E = gate_w.shape[1]
        x = hidden_states.reshape(-1, H)
        T = x.shape[0]
        K = TOP_K
        P = T * K
        C = 2 * (P // E)
        probs = jax.nn.softmax(x @ gate_w, axis=-1)
        w, sel = jax.lax.top_k(probs, K)
        w = w / jnp.sum(w, axis=-1, keepdims=True)
        flat_e = sel.reshape(-1)
        flat_t = jnp.repeat(jnp.arange(T), K)
        flat_w = w.reshape(-1)
        order = jnp.argsort(flat_e)
        se = flat_e[order]
        start = jnp.searchsorted(se, jnp.arange(E))
        pos = jnp.arange(P) - start[se]
        slot = jnp.where(pos < C, se * C + pos, E * C)
        slot_pair = jnp.full((E * C,), P, dtype=jnp.int32).at[slot].set(order.astype(jnp.int32), mode='drop')
        t_slot = jnp.concatenate([flat_t, jnp.array([T])])[slot_pair]
        w_slot = jnp.concatenate([flat_w, jnp.zeros((1,), flat_w.dtype)])[slot_pair]
        x_pad = jnp.concatenate([x, jnp.zeros((1, H), x.dtype)], axis=0)
        xg = x_pad[t_slot].reshape(E, C, H)
        g = jnp.einsum('ech,ehi->eci', xg, w_gate)
        u = jnp.einsum('ech,ehi->eci', xg, w_up)
        y = jnp.einsum('eci,eih->ech', jax.nn.silu(g) * u, w_down).reshape(E * C, H)
        out = jnp.zeros((T + 1, H), x.dtype).at[t_slot].add(w_slot[:, None] * y)
        return out[:T].reshape(B, S, H)
    x = x + _L0_xattn_ref(_layernorm(x, axis=-1), ctx_512, ctx_512)
    x = x + _L0_ffn_ref(_layernorm(x, axis=-1), L0_ffn_gate_w, L0_ffn_w_gate, L0_ffn_w_up, L0_ffn_w_down)
    return x

_drawn_inputs = setup_inputs


def setup_inputs(seed=0):
    import zlib

    import numpy as np

    out = dict(_drawn_inputs(seed))
    spreads = {}
    factors = {}
    for name, (base, spread) in spreads.items():
        noise = np.random.default_rng([zlib.crc32(name.encode()), seed]).standard_normal(out[name].shape)
        drawn = base * np.exp(spread * noise) if base else spread * noise
        out[name] = jnp.asarray(drawn.astype(out[name].dtype))
    for name, factor in factors.items():
        out[name] = (out[name] * factor).astype(out[name].dtype)
    return out
```

```python
from contextlib import ExitStack

import numpy as np

import concourse.bass as bass
from concourse import mybir

F32 = mybir.dt.float32
F32R = mybir.dt.float32r
BF16 = mybir.dt.bfloat16
I32 = mybir.dt.int32
U32 = mybir.dt.uint32
ALU = mybir.AluOpType
ACT = mybir.ActivationFunctionType
AX = mybir.AxisListType

P = 128
B, S, E = 64, 64, 256
KV, G, D = 8, 4, 8
T = B * S
NT = T // P
NX, K, I = 32, 8, 96
CAP = 2 * (T * K // NX)
REGION = T + P
NULL = NX * REGION
ROW = E + NX + 1
NB = -(-(T * K // P + NX) // 8) * 8
NS = NB // 2
KEY0 = 1 << 18
EPS = 1e-5
SCALE = float(D) ** -0.5
NACC = 4
VC = D + 1
WG = 4

CONST_COLS = {}
_at = 0
for _name, _width in (("ident", P), ("tri", P), ("gmask", 2), ("ebase", NX), ("key0", NX), ("tok", 2), ("pad", 1),
                      ("tile", NB // P + 1), ("steps", CAP // P), ("ones", P)):
    CONST_COLS[_name] = slice(_at, _at + _width)
    _at += _width
NCONST = _at
NCH = NB // P + 1


def constants():
    c = np.zeros((P, NCONST), np.float32)
    p = np.arange(P)[:, None]
    c[:, CONST_COLS["ident"]] = p == np.arange(P)
    c[:, CONST_COLS["tri"]] = p < np.arange(P)
    c[:, CONST_COLS["gmask"]] = (p % 16) // 8 == np.arange(2)
    c[:, CONST_COLS["ebase"]] = np.arange(NX) * REGION
    c[:, CONST_COLS["key0"]] = KEY0 - np.arange(NX) * REGION
    c[:, CONST_COLS["tok"]] = p + P * np.arange(2) - 2 * P
    c[:, CONST_COLS["pad"]] = T + p
    c[:, CONST_COLS["tile"]] = p + P * np.arange(NCH)
    c[:, CONST_COLS["steps"]] = P * np.arange(CAP // P)
    c[:, CONST_COLS["ones"]] = 1.0
    return c


class Step:

    def __init__(self, q, r, ring):
        self.q, self.r, self.ring = q, r, ring

    def at(self, d):
        return Step(self.q + (self.r + d) // self.ring, (self.r + d) % self.ring, self.ring)

    @property
    def n(self):
        return self.q * self.ring + self.r

    def within(self, count):
        return not isinstance(self.q, int) or 0 <= self.n < count


def run_frames(eng, frame, ring, first, loop_from, loop_to, last):
    for n in range(first, loop_from):
        frame(Step(n // ring, n % ring, ring))
    with eng.Fori(loop_from // ring, loop_to // ring) as i:
        for k in range(ring):
            frame(Step(i, k, ring))
    for n in range(loop_to, last + 1):
        frame(Step(n // ring, n % ring, ring))


def due(value):
    return not isinstance(value, int) or value > 0


def at_most(value, most):
    return min(value, most) if isinstance(value, int) else value


def settle(eng, turns):
    eng.sem_inc(turns, 1)


def build(nc, x, ctx_in, gate_w, w_gate, w_up, w_down, const, out):
    xf = x.rearrange("b s e -> (b s) e")
    cf = ctx_in.rearrange("b s e -> (b s) e")
    outf = out.rearrange("b s e -> (b s) e")
    table = nc.dram_tensor("table", (NULL + P, ROW), F32, kind="Internal").ap()
    acc = [nc.dram_tensor(f"acc{i}", (T + P, E), F32, kind="Internal").ap() for i in range(NACC)]

    with ExitStack() as stack:
        def sem(name):
            return stack.enter_context(nc.semaphore(name))

        def sems(name, n):
            return [sem(f"{name}{i}") for i in range(n)]

        def allocate(where):
            def sb(name, shape, dt=F32):
                return where.enter_context(nc.sbuf_tensor(name, shape, dt))
            return sb

        sb = allocate(stack)
        con = sb("con", [P, NCONST])
        tri_b = sb("tri_b", [P, P], BF16)
        ones_b = sb("ones_b", [P, P], BF16)
        gw = sb("gw", [P, 2, NX])
        pad_row = sb("pad_row", [P, ROW])
        key_base = sb("key_base", [P, NX])
        w_gu = [sb(f"w_gu_{x}", [P, 2, NX * 2 * I], F32R) for x in ("hi", "lo")]
        stage = [sb(f"stage{i}", [P, 2, WG, 2 * I]) for i in range(2)]
        tile_rows = sb("tile_rows", [1, 2 * NCH * P], I32)
        pad_at = sb("pad_at", [1, NX], I32)

        def cc(name):
            return con[:, CONST_COLS[name]]
        ident = cc("ident")

        phase_a = ExitStack()
        sb = allocate(phase_a)
        x_q = [sb(f"x_q{i}", [P, E]) for i in range(2)]
        x_r = [sb(f"x_r{i}", [P, E]) for i in range(2)]
        ctx_t = [sb(f"ctx_t{i}", [P, KV * D]) for i in range(2)]
        ctx_v = [sb(f"ctx_v{i}", [P, 2, KV * D]) for i in range(2)]
        q_n = sb("q_n", [P, E])
        q_parts = sb("q_parts", [P, 8, 2, 4, 16])
        k_parts = sb("k_parts", [P, 4, 2, 2, 4 * D])
        q_t = [sb(f"q_t{i}", [P, 8, 3 * S], F32R) for i in range(2)]
        k_t = [sb(f"k_t{i}", [P, 8, 2, S], F32R) for i in range(2)]
        v_t = [sb(f"v_t{i}", [P, 2, KV, 2 * VC]) for i in range(2)]
        s_max = [sb(f"s_max{i}", [P, 16]) for i in range(2)]
        s_sub = [sb(f"s_sub{i}", [P, 16, S]) for i in range(2)]
        probs = [sb(f"probs{i}", [P, 8, P]) for i in range(2)]
        inv = sb("inv", [P, KV * G])
        att = sb("att", [P, E])
        x1 = [sb(f"x1_{i}", [P, E]) for i in range(2)]
        stats = sb("stats", [P, 2, 6])
        mean_var = sb("mean_var", [P, 2, 2])
        var_eps = sb("var_eps", [P, 2])
        half = sb("half", [P, 2])
        rstd = sb("rstd", [P, 2])
        shift = sb("shift", [P, 2])
        row = [sb(f"row{i}", [P, ROW]) for i in range(2)]
        x2_t = sb("x2_t", [P, 2, P])
        top = sb("top", [P, 8])
        neg_top = sb("neg_top", [P, 1])
        logits = sb("logits", [P, NX])
        ex = sb("ex", [P, NX])
        without = sb("without", [P, NX])
        mask = sb("mask", [P, NX], BF16)
        chosen = sb("chosen", [P, NX])
        w_sum = sb("w_sum", [P, 1])
        w_inv = sb("w_inv", [P, 1])
        key_free = sb("key_free", [P, NX])
        key = sb("key", [P, NX])
        key8 = sb("key8", [P, 8])
        slot = [sb(f"slot{i}", [P, 8], U32) for i in range(2)]
        zeros = sb("zeros", [P, E * (T + P) // P // 3])
        count = sb("count", [P, NX])
        count_le = sb("count_le", [P, NX, CAP // P])
        tiles = sb("tiles", [P, NX])
        tiles_end = sb("tiles_end", [P, NX])
        past = sb("past", [P, NCH, NX])
        past_tiles = sb("past_tiles", [P, NCH, NX])
        expert = sb("expert", [P, NCH])
        begun = sb("begun", [P, NCH])
        live = sb("live", [P, NCH])
        inside = sb("inside", [P, NCH])
        values = sb("values", [P, 2, NCH])
        pad_f = sb("pad_f", [P, NX])
        phase_a.close()

        phase_b = ExitStack()
        sb = allocate(phase_b)
        w_dn = [sb(f"w_dn_{x}", [I, NX * E], F32R) for x in ("hi", "lo")]
        rows = [sb(f"rows{i}", [P, 2, ROW]) for i in range(2)]
        x_t = [[sb(f"x_t_{x}{i}", [P, 2, 2, P], F32R) for i in range(2)] for x in ("hi", "lo")]
        gated = [sb(f"gated{i}", [P, 2, I]) for i in range(2)]
        inner = [sb(f"inner{i}", [P, 2, I]) for i in range(2)]
        h_t = [[sb(f"h_t_{x}{i}", [I, 2, P], F32R) for i in range(2)] for x in ("hi", "lo")]
        y = [sb(f"y{i}", [P, 2, E]) for i in range(4)]
        weight = [sb(f"weight{i}", [P, 2]) for i in range(2)]
        tokens = [sb(f"tokens{i}", [P, 2], U32) for i in range(4)]
        phase_b.close()
        phase_c = ExitStack()
        sb = allocate(phase_c)
        CR = 4
        part = [[sb(f"part{i}_{a}", [P, CR * E]) for a in range(NACC)] for i in range(2)]
        phase_c.close()

        psum = stack.enter_context(nc.psum_tensor("psum", [P, 8, 512], F32))

        def bank(n, k=1):
            return psum[:, n:n + k, :].rearrange("p k c -> p (k c)")
        scores_p = [bank(0, 2), bank(2, 2)]
        sub_t_p = bank(4, 2)
        turn_p = bank(6)
        out_p = bank(7)[:, 0:KV * G * VC].rearrange("p (h c) -> p h c", c=VC)
        logits_p = turn_p[:, 0:NX]
        before_p = turn_p[:, 0:NX]
        tile_p = turn_p[:, NX:2 * NX]
        x_t_p = [bank(0), bank(1)]
        gu_p = [bank(2), bank(3)]
        h_t_p = bank(4)
        y_p = [bank(5), bank(6)]

        def key_view(jj, low):
            return k_parts[:, :, jj, low, :].rearrange("t jp (x d) -> t jp x d", d=D)

        def key_source(k, jj):
            return (ctx_t[k][:, 32 * jj:32 * jj + 32].rearrange("t (jp d) -> t jp d", d=D).unsqueeze(2)
                    .broadcast_to([P, 4, 4, D]))

        def query_source(jj):
            return (q_n[:, P * jj:P * jj + P].rearrange("t (n f) -> t n f", f=16).unsqueeze(2)
                    .broadcast_to([P, 8, 2, 16]))

        pool_turns = sem("pool_turns")
        dve_turns = sem("dve_turns")
        pe_turns = sem("pe_turns")
        consts_in = sem("consts_in")
        consts_made = sem("consts_made")
        ones_made = sem("ones_made")
        pool_ready = sem("pool_ready")
        stage_in = sems("stage_in", 2)
        stage_hi = sem("stage_hi")
        stage_lo = sem("stage_lo")
        x_q_in = sems("x_q_in", 2)
        x_r_in = sems("x_r_in", 2)
        ctx_in_s = sems("ctx_in_s", 2)
        ctx_v_in = sems("ctx_v_in", 2)
        x1_out = sems("x1_out", 2)
        zero_out = sem("zero_out")
        null_out = sem("null_out")
        k_hi = sem("k_hi")
        k_lo = sem("k_lo")
        k_turned = sem("k_turned")
        k_masked = sem("k_masked")
        v_copied = sem("v_copied")
        scored = sems("scored", 2)
        max_made = sems("max_made", 2)
        sub_made = sems("sub_made", 2)
        sub_turned = sems("sub_turned", 2)
        probs_made = sems("probs_made", 2)
        attended = sems("attended", 2)
        stats1 = sem("stats1")
        stats2 = sem("stats2")
        aggr1 = sem("aggr1")
        aggr2 = sem("aggr2")
        var_made = sem("var_made")
        rstd_made = sem("rstd_made")
        shift_made = sem("shift_made")
        inv_made = sem("inv_made")
        att_made = sem("att_made")
        x1_made = sem("x1_made")
        q_normed = sem("q_normed")
        q_hi = sem("q_hi")
        q_lo = sem("q_lo")
        q_turned = sems("q_turned", 2)
        q_copied = sems("q_copied", 2)
        row_normed = sem("row_normed")
        row_weighted = sem("row_weighted")
        row_named = sem("row_named")
        x2_turned = sem("x2_turned")
        x2_copied = sem("x2_copied")
        logits_made = sem("logits_made")
        logits_copied = sem("logits_copied")
        top_made = sem("top_made")
        neg_made = sem("neg_made")
        ex_made = sem("ex_made")
        without_made = sem("without_made")
        mask_made = sem("mask_made")
        chosen_made = sem("chosen_made")
        w_inv_made = sem("w_inv_made")
        counted = sem("counted")
        free_made = sem("free_made")
        key_made = sem("key_made")
        base_moved = sem("base_moved")
        key8_made = sem("key8_made")
        slots_made = sem("slots_made")
        sent = sems("sent", 2)
        routed = sem("routed")
        table_step = sem("table_step")
        values_made = sem("values_made")
        values_turned = sem("values_turned")
        tiles_known = sem("tiles_known")
        pads_out = sem("pads_out")

        rows_in = sems("rows_in", 2)
        x_turned = sem("x_turned")
        x_hi = sem("x_hi")
        x_lo = sem("x_lo")
        weight_made = sem("weight_made")
        tokens_made = sem("tokens_made")
        gu_made = sem("gu_made")
        gated_made = sem("gated_made")
        inner_made = sem("inner_made")
        h_turned = sem("h_turned")
        h_hi = sem("h_hi")
        h_lo = sem("h_lo")
        y_made = sem("y_made")
        y_copied = sem("y_copied")
        added = sems("added", NACC)
        part_in = sems("part_in", 2)
        half_sum = sems("half_sum", 2)
        summed = sem("summed")
        out_done = sems("out_done", 2)

        NGRP = NX // WG
        block = stack.enter_context(nc.Block())

        @block.sync
        def _(sp):
            sp.dma_start(con[:, :], const).then_inc(consts_in, 16)
            sp.dma_start(gw[:, :, :], gate_w.rearrange("(c p) e -> p c e", p=P)).then_inc(consts_in, 16)

            def load_gate_up(g):
                if due(g - 1):
                    sp.wait_ge(stage_lo, g - 1)
                for c in range(2):
                    for k, w in enumerate((w_gate, w_up)):
                        sp.dma_start(stage[g % 2][:, c, :, k * I:(k + 1) * I],
                                     w[WG * g:WG * g + WG, c * P:(c + 1) * P, :].rearrange("e p i -> p e i")
                                     ).then_inc(stage_in[g % 2], 16)

            def load_front(t):
                k = t.r
                if due(t.n - 1):
                    sp.wait_ge(q_normed, t.n - 1)
                sp.dma_start(x_q[k][:, :], xf[bass.ds(t.n * P, P), :]).then_inc(x_q_in[k], 16)
                if due(t.n - 1):
                    sp.wait_ge(k_lo, t.n - 1)
                sp.dma_start(ctx_t[k][:, :], cf[bass.ds(t.n * P, P), :]).then_inc(ctx_in_s[k], 16)
                if due(t.n - 1):
                    sp.wait_ge(v_copied, t.n - 1)
                for g in range(2):
                    sp.dma_start(ctx_v[k][S * g:S * g + S, :, :],
                                 cf[bass.ds(t.n * P, P), :].rearrange("(b t) f -> t b f", b=2)
                                 ).then_inc(ctx_v_in[k], 16)

            def frame(t):
                if t.at(2).within(NT):
                    load_front(t.at(2))
                if t.within(NT):
                    if due(t.n - 1):
                        sp.wait_ge(x1_made, t.n - 1)
                    sp.dma_start(x_r[t.r][:, :], xf[bass.ds(t.n * P, P), :]).then_inc(x_r_in[t.r], 16)
                if t.at(-1).within(NT):
                    u = t.at(-1)
                    sp.wait_ge(x1_made, u.n + 1)
                    sp.dma_start(acc[0][bass.ds(u.n * P, P), :], x1[u.r][:, :]).then_inc(x1_out[u.r], 16)

            frame(Step(-1, 0, 2))
            frame(Step(-1, 1, 2))
            for g in range(NGRP):
                load_gate_up(g)
            sp.wait_ge(pool_ready, 3)
            for a in range(1, NACC):
                for n in range(3):
                    step = (T + P) // P // 3
                    sp.dma_start(acc[a].rearrange("(p r) e -> p r e", p=P)[:, n * step:(n + 1) * step, :],
                                 zeros[:, :].rearrange("p (r e) -> p r e", e=E)).then_inc(zero_out, 16)
            sp.dma_start(acc[0][T:T + P, :], zeros[:, 0:E]).then_inc(zero_out, 16)
            sp.dma_start(table[NULL:NULL + P, :], pad_row[:, :]).then_inc(null_out, 16)
            run_frames(sp, frame, 2, 0, 2, 28, NT)

            def load_down(g):
                if due(NGRP + g - 1):
                    sp.wait_ge(stage_lo, NGRP + g - 1)
                sp.dma_start(stage[g % 2][0:I, :, :, :].rearrange("i c e w -> i (c e w)")[:, 0:WG * E]
                             .rearrange("i (e h) -> i e h", h=E),
                             w_down[WG * g:WG * g + WG, :, :].rearrange("e i h -> i e h")
                             ).then_inc(stage_in[g % 2], 16)
            load_down(0)
            load_down(1)

            for k in range(2):
                sp.wait_ge(sent[k], 16 * K * (NT // 2))
                sp.wait_ge(x1_out[k], 16 * (NT // 2))
            sp.wait_ge(tiles_known, 2)
            with sp.Fori(0, NX) as e:
                at = sp.value_load(pad_at[0:1, bass.ds(e, 1)], min_val=0, max_val=NULL - P)
                sp.dma_start(table[bass.ds(at, P), :], pad_row[:, :]).then_inc(pads_out, 16)
            for g in range(2, NGRP):
                load_down(g)
            sp.wait_ge(pads_out, 16 * NX)
            sp.wait_ge(null_out, 16)

            def load_rows(s):
                if due(s.n - 1):
                    sp.wait_ge(x_turned, s.n - 1)
                if due(s.n - 1):
                    sp.wait_ge(tokens_made, s.n - 1)
                for i in range(2):
                    at = sp.value_load(tile_rows[0:1, bass.ds(s.n * 2 + i, 1)], min_val=0, max_val=NULL)
                    sp.dma_start(rows[s.r % 2][:, i, :], table[bass.ds(at, P), :]).then_inc(rows_in[s.r % 2], 16)

            run_frames(sp, load_rows, 4, 0, 4, NS, NS - 1)

            for a in range(NACC):
                sp.wait_ge(added[a], 16 * NB // NACC)
            sp.wait_ge(zero_out, 16 * (3 * (NACC - 1) + 1))
            chunks = [[a_[0:T, :].rearrange("(p r) e -> p (r e)", p=P)[:, n * CR * E:(n + 1) * CR * E] for a_ in acc]
                      for n in range(T // P // CR)]
            final = [outf.rearrange("(p r) e -> p (r e)", p=P)[:, n * CR * E:(n + 1) * CR * E]
                     for n in range(T // P // CR)]
            for n in range(len(chunks) + 1):
                if n < len(chunks):
                    if due(16 * (n // 2)):
                        sp.wait_ge(out_done[n % 2], 16 * (n // 2))
                    for a in range(NACC):
                        sp.dma_start(part[n % 2][a][:, :], chunks[n][a]).then_inc(part_in[n % 2], 16)
                if n >= 1:
                    if due(n):
                        sp.wait_ge(summed, n)
                    sp.dma_start(final[n - 1], part[(n - 1) % 2][0][:, :]).then_inc(out_done[(n - 1) % 2], 16)
            for k in range(2):
                sp.wait_ge(out_done[k], 16 * len(chunks) // 2)

        @block.gpsimd
        def _(pool):
            turns = pool_turns
            pool.memset(zeros[:, :], 0.0).then_inc(pool_ready, 1)
            pool.memset(half[:, :], -0.5).then_inc(pool_ready, 1)
            pool.wait_ge(consts_made, 7)
            pool.memset(pad_row[:, 0:ROW - 1], 0.0).then_inc(pool_ready, 1)
            pool.wait_ge(pool_ready, 3)

            def frame(t):
                if t.within(NT + 1) or t.at(1).within(NT):
                    lo = 0 if t.at(-1).within(NT) else 1
                    hi = 2 if t.at(1).within(NT) else 1
                    if lo < hi:
                        pool.wait_ge(var_made, t.n + 2)
                        if due(t.n + 1):
                            pool.wait_ge(shift_made, t.n + 1)
                        if due(t.n - 1):
                            pool.wait_ge(row_normed, t.n - 1)
                        if due(at_most(t.n + 1, NT)):
                            pool.wait_ge(q_normed, at_most(t.n + 1, NT))
                        pool.tensor_tensor(rstd[:, lo:hi], var_eps[:, lo:hi], half[:, lo:hi],
                                           ALU.pow).then_inc(rstd_made, 1)
                if t.at(-2).within(NT):
                    u = t.at(-2)
                    pool.wait_ge(slots_made, u.n + 1)
                    pool.wait_ge(row_weighted, u.n + 1)
                    pool.wait_ge(row_named, u.n + 1)
                    pool.wait_ge(row_normed, u.n + 1)
                    settle(pool, turns)
                    for k in range(K):
                        pool.indirect_dma_start(out=table[:, :],
                                                out_offset=bass.IndirectOffsetOnAxis(ap=slot[u.r][:, k:k + 1], axis=0),
                                                in_=row[u.r][:, :], in_offset=None).then_inc(sent[u.r], 16)
            run_frames(pool, frame, 2, -1, 2, 30, NT + 1)

            pool.wait_ge(zero_out, 16 * (3 * (NACC - 1) + 1))
            for k in range(2):
                pool.wait_ge(x1_out[k], 16 * (NT // 2))

            def add(s):
                for i in range(2):
                    a = (2 * s.r + i) % NACC
                    if due(16 * (s.q * 2 + s.r // 2)):
                        pool.wait_ge(added[a], 16 * (s.q * 2 + s.r // 2))
                    pool.wait_ge(y_copied, s.n + 1)
                    settle(pool, turns)
                    pool.indirect_dma_start(out=acc[a][:, :],
                                            out_offset=bass.IndirectOffsetOnAxis(ap=tokens[s.r][:, i:i + 1], axis=0),
                                            in_=y[s.r][:, i, :], in_offset=None,
                                            compute_op=ALU.add).then_inc(added[a], 16)
            run_frames(pool, add, 4, 0, 4, NS, NS - 1)

        @block.scalar
        def _(act):
            for g in range(NGRP):
                act.wait_ge(stage_in[g % 2], 64 * (g // 2 + 1))
                wide = slice(WG * 2 * I * g, WG * 2 * I * (g + 1))
                act.copy(w_gu[0][:, :, wide],
                         stage[g % 2][:, :, :, :].rearrange("p c e w -> p c (e w)")).then_inc(stage_hi, 1)
            act.wait_ge(consts_in, 32)
            act.wait_ge(ones_made, 6)

            def frame(t):
                front, rear = t.at(1), t.at(-1)
                if front.within(NT):
                    k = front.r
                    act.wait_ge(ctx_in_s[k], 16 * (front.q + 1))
                    if due(front.n):
                        act.wait_ge(k_turned, front.n)
                    for jj in range(2):
                        last = act.copy(key_view(jj, 0).bitcast(F32R), key_source(k, jj))
                    last.then_inc(k_hi, 1)
                    act.wait_ge(ctx_v_in[k], 32 * (front.q + 1))
                    for u in range(2):
                        if due(front.n - 1):
                            act.wait_ge(attended[u], front.n - 1)
                    for g in range(2):
                        half_p = slice(S * g, S * g + S)
                        last = act.copy(v_t[k][half_p, :, :, VC * g:VC * g + D].rearrange("t b j d -> t (b j) d"),
                                        ctx_v[k][half_p, :, :].rearrange("t b (j d) -> t (b j) d", d=D))
                    last.then_inc(v_copied, 1)
                    act.wait_ge(k_turned, front.n + 1)
                    for u in range(2):
                        if due(front.n - 1):
                            act.wait_ge(scored[u], front.n - 1)
                    for g in range(2):
                        last = act.activation(k_t[k][:, :, g, :], turn_p.rearrange("r (x t) -> r x t", t=S),
                                              ACT.Copy, scale=cc("gmask")[:, g:g + 1])
                    last.then_inc(k_masked, 1)

                def probabilities(u):
                    act.wait_ge(sub_turned[u], t.n + 1)
                    if due(t.n):
                        act.wait_ge(attended[u], t.n)
                    act.activation(probs[u][:, :, :].rearrange("p x s -> p (x s)"), sub_t_p,
                                   ACT.Exp, scale=SCALE).then_inc(probs_made[u], 1)
                if t.within(NT):
                    probabilities(0)
                if rear.within(NT):
                    k = rear.r
                    act.wait_ge(shift_made, t.n + 2)
                    if due(16 * K * rear.q):
                        act.wait_ge(sent[k], 16 * K * rear.q)
                    act.activation(row[k][:, 0:E], x1[k][:, :], ACT.Identity, bias=shift[:, 0:1],
                                   scale=rstd[:, 0:1]).then_inc(row_normed, 1)
                if front.within(NT):
                    k = front.r
                    act.wait_ge(shift_made, t.n + 2)
                    if due(front.n):
                        act.wait_ge(q_lo, front.n)
                    act.activation(q_n[:, :], x_q[k][:, :], ACT.Identity, bias=shift[:, 1:2],
                                   scale=rstd[:, 1:2]).then_inc(q_normed, 1)
                    act.wait_ge(q_normed, front.n + 1)
                    for u in range(2):
                        if due(front.n):
                            act.wait_ge(q_turned[u], front.n)
                    for jj in range(2):
                        last = act.copy(q_parts[:, :, jj, 0:4:2, :].bitcast(F32R), query_source(jj))
                    last.then_inc(q_hi, 1)
                if rear.within(NT):
                    act.wait_ge(x2_turned, rear.n + 1)
                    if due(rear.n):
                        act.wait_ge(logits_made, rear.n)
                    act.copy(x2_t[:, :, :].rearrange("p c t -> p (c t)"), turn_p[:, 0:E]).then_inc(x2_copied, 1)
                    act.wait_ge(neg_made, rear.n + 1)
                    if due(rear.n):
                        act.wait_ge(chosen_made, rear.n)
                    act.activation(ex[:, :], logits[:, :], ACT.Exp, bias=neg_top[:, 0:1]).then_inc(ex_made, 1)
                if t.within(NT):
                    probabilities(1)
                if front.within(NT):
                    for u in range(2):
                        act.wait_ge(q_turned[u], front.n + 1)
                        if due(front.n - 1):
                            act.wait_ge(scored[u], front.n - 1)
                        src = turn_p.rearrange("r (c b s) -> r c b s", b=2, s=S)
                        dst = q_t[front.r][:, 4 * u:4 * u + 4, :].rearrange("r c (b s) -> r c b s", b=3)[:, :, 0:3:2, :]
                        act.copy(dst, src).then_inc(q_copied[u], 1)

            run_frames(act, frame, 2, -1, 2, 30, NT)

            act.wait_ge(routed, 2)
            for k in range(2):
                act.wait_ge(sent[k], 16 * K * (NT // 2))
                act.wait_ge(x1_out[k], 16 * (NT // 2))
            act.wait_ge(zero_out, 16 * (3 * (NACC - 1) + 1))
            for g in range(NGRP):
                act.wait_ge(stage_in[g % 2], 16 * 4 * (NGRP // 2) + 16 * (g // 2 + 1))
                act.copy(w_dn[0][:, WG * E * g:WG * E * (g + 1)],
                         stage[g % 2][0:I, :, :, :].rearrange("i c e w -> i (c e w)")[:, 0:WG * E]
                         ).then_inc(stage_hi, 1)

            def frame_b(s):
                f, h, b = s.at(1), s.at(-1), s.at(-2)
                if f.within(NS):
                    act.wait_ge(x_turned, f.n + 1)
                    if due(f.n - 1):
                        act.wait_ge(gu_made, f.n - 1)
                    act.copy(x_t[0][f.r % 2][:, :, :, :].rearrange("p i c t -> p (i c t)"),
                             x_t_p[f.r % 2]).then_inc(x_hi, 1)
                if s.within(NS):
                    act.wait_ge(gu_made, s.n + 1)
                    if due(s.n - 1):
                        act.wait_ge(inner_made, s.n - 1)
                    act.activation(gated[s.r % 2][:, :, :],
                                   gu_p[s.r % 2][:, 0:4 * I].rearrange("p (i w) -> p i w", i=2)[:, :, 0:I],
                                   ACT.Silu).then_inc(gated_made, 1)
                if h.within(NS):
                    act.wait_ge(h_turned, h.n + 1)
                    if due(h.n - 1):
                        act.wait_ge(y_made, h.n - 1)
                    act.copy(h_t[0][h.r % 2][:, :, :].rearrange("i k t -> i (k t)"),
                             h_t_p[0:I, 0:2 * P]).then_inc(h_hi, 1)
                if b.within(NS):
                    act.wait_ge(y_made, b.n + 1)
                    for i in range(2):
                        if due(16 * (b.q * 2 + b.r // 2 - 1)):
                            act.wait_ge(added[(2 * b.r + i) % NACC], 16 * (b.q * 2 + b.r // 2 - 1))
                    act.copy(y[b.r][:, :, :].rearrange("p i e -> p (i e)"), y_p[b.r % 2]).then_inc(y_copied, 1)
            run_frames(act, frame_b, 4, -1, 4, NS - 4, NS + 1)

        @block.vector
        def _(dve):
            turns = dve_turns
            dve.wait_ge(consts_in, 32)
            dve.tensor_copy(tri_b[:, :], cc("tri")).then_inc(consts_made, 1)
            dve.tensor_copy(ones_b[:, :], cc("ones")).then_inc(consts_made, 1)
            dve.tensor_copy(key_base[:, :], cc("key0")).then_inc(consts_made, 1)
            dve.tensor_copy(pad_row[:, ROW - 1:ROW].bitcast(U32), cc("pad")).then_inc(consts_made, 1)
            for k in range(2):
                dve.tensor_copy(row[k][:, ROW - 1:ROW].bitcast(I32), cc("tok")[:, k:k + 1]).then_inc(consts_made, 1)
            dve.memset(stats[:, :, :], 0.0).then_inc(consts_made, 1)
            for k in range(2):
                dve.memset(q_t[k][:, :, S:2 * S].bitcast(F32), 0.0).then_inc(ones_made, 1)
                dve.memset(v_t[k][:, :, :, :], 0.0).then_inc(ones_made, 1)
            dve.wait_ge(ones_made, 4)
            for k in range(2):
                for g in range(2):
                    last = dve.memset(v_t[k][S * g:S * g + S, :, :, VC * g + D:VC * g + VC], 1.0)
                last.then_inc(ones_made, 1)
            for g in range(NGRP):
                if due(g + 1):
                    dve.wait_ge(stage_hi, g + 1)
                wide = slice(WG * 2 * I * g, WG * 2 * I * (g + 1))
                dve.tensor_tensor(w_gu[1][:, :, wide], stage[g % 2][:, :, :, :].rearrange("p c e w -> p c (e w)"),
                                  w_gu[0][:, :, wide].bitcast(F32), ALU.subtract).then_inc(stage_lo, 1)

            def frame(t):
                front, rear = t.at(1), t.at(-1)

                def unit_max(u):
                    dve.wait_ge(scored[u], t.n + 1)
                    if due(t.n):
                        dve.wait_ge(sub_made[u], t.n)
                    dve.tensor_reduce(s_max[u][:, :], scores_p[u].rearrange("p (x t) -> p x t", t=S),
                                      AX.X, ALU.max).then_inc(max_made[u], 1)

                def unit_sub(u):
                    dve.wait_ge(max_made[u], t.n + 1)
                    if due(t.n):
                        dve.wait_ge(sub_turned[u], t.n)
                    dve.tensor_tensor(s_sub[u][:, :, :], scores_p[u].rearrange("p (x t) -> p x t", t=S),
                                      s_max[u][:, :].unsqueeze(2).broadcast_to([P, 16, S]),
                                      ALU.subtract).then_inc(sub_made[u], 1)
                if t.within(NT):
                    unit_max(0)
                    unit_sub(0)
                lo = 0 if rear.within(NT) else 1
                hi = 2 if front.within(NT) else 1
                if front.within(NT):
                    k = front.r
                    dve.wait_ge(x_q_in[k], 16 * (front.q + 1))
                    if due(front.n):
                        dve.wait_ge(aggr1, front.n)
                    dve.bn_stats(stats[:, 1, :], x_q[k][:, :]).then_inc(stats1, 1)
                if rear.within(NT):
                    k = rear.r
                    for u in range(2):
                        dve.wait_ge(attended[u], rear.n + 1)
                    if due(rear.n):
                        dve.wait_ge(att_made, rear.n)
                    dve.reciprocal(inv[:, :], out_p[:, :, D]).then_inc(inv_made, 1)
                    dve.wait_ge(inv_made, rear.n + 1)
                    if due(rear.n):
                        dve.wait_ge(x1_made, rear.n)
                    dve.tensor_tensor(att[:, :].rearrange("p (h d) -> p h d", d=D), out_p[:, :, 0:D],
                                      inv[:, :].unsqueeze(2).broadcast_to([P, KV * G, D]),
                                      ALU.mult).then_inc(att_made, 1)
                    dve.wait_ge(att_made, rear.n + 1)
                    dve.wait_ge(x_r_in[k], 16 * (rear.q + 1))
                    if due(16 * rear.q):
                        dve.wait_ge(x1_out[k], 16 * rear.q)
                    if due(rear.n - 1):
                        dve.wait_ge(row_normed, rear.n - 1)
                    dve.tensor_tensor(x1[k][:, :], att[:, :], x_r[k][:, :], ALU.add).then_inc(x1_made, 1)
                if front.within(NT):
                    dve.wait_ge(stats1, front.n + 1)
                    if due(front.n):
                        dve.wait_ge(shift_made, front.n)
                    settle(dve, turns)
                    dve.bn_aggr(mean_var[:, 1, :], stats[:, 1, :]).then_inc(aggr1, 1)
                if rear.within(NT):
                    dve.wait_ge(x1_made, rear.n + 1)
                    if due(rear.n):
                        dve.wait_ge(aggr2, rear.n)
                    dve.bn_stats(stats[:, 0, :], x1[rear.r][:, :]).then_inc(stats2, 1)
                    dve.wait_ge(stats2, rear.n + 1)
                    if due(t.n + 1):
                        dve.wait_ge(shift_made, t.n + 1)
                    settle(dve, turns)
                    dve.bn_aggr(mean_var[:, 0, :], stats[:, 0, :]).then_inc(aggr2, 1)
                    dve.wait_ge(aggr2, rear.n + 1)
                if lo < hi:
                    if front.within(NT):
                        dve.wait_ge(aggr1, front.n + 1)
                    if due(t.n + 1):
                        dve.wait_ge(rstd_made, t.n + 1)
                    dve.tensor_scalar(var_eps[:, lo:hi], mean_var[:, lo:hi, 1], EPS, None,
                                      ALU.add).then_inc(var_made, 1)
                if t.within(NT):
                    unit_max(1)
                if front.within(NT):
                    dve.wait_ge(k_hi, front.n + 1)
                    for jj in range(2):
                        last = dve.tensor_tensor(key_view(jj, 1).bitcast(F32R), key_source(front.r, jj),
                                                 key_view(jj, 0), ALU.subtract)
                    last.then_inc(k_lo, 1)
                if lo < hi:
                    dve.wait_ge(rstd_made, t.n + 2)
                    if due(rear.n):
                        dve.wait_ge(row_normed, rear.n)
                    if due(at_most(t.n + 1, NT)):
                        dve.wait_ge(q_normed, at_most(t.n + 1, NT))
                    dve.scalar_tensor_tensor(out=shift[:, lo:hi], in0=mean_var[:, lo:hi, 0], scalar=-1.0,
                                             in1=rstd[:, lo:hi], op0=ALU.mult, op1=ALU.mult).then_inc(shift_made, 1)
                if t.within(NT):
                    unit_sub(1)
                if front.within(NT):
                    dve.wait_ge(q_hi, front.n + 1)
                    for jj in range(2):
                        last = dve.tensor_tensor(q_parts[:, :, jj, 1:4:2, :].bitcast(F32R), query_source(jj),
                                                 q_parts[:, :, jj, 0:4:2, :], ALU.subtract)
                    last.then_inc(q_lo, 1)
                if rear.within(NT):
                    k = rear.r
                    dve.wait_ge(logits_made, rear.n + 1)
                    if due(rear.n):
                        dve.wait_ge(ex_made, rear.n)
                    dve.tensor_copy(logits[:, :], logits_p).then_inc(logits_copied, 1)
                    dve.wait_ge(logits_copied, rear.n + 1)
                    settle(dve, turns)
                    dve.max(top[:, :], logits[:, :]).then_inc(top_made, 1)
                    dve.wait_ge(top_made, rear.n + 1)
                    dve.tensor_scalar(neg_top[:, :], top[:, 0:1], -1.0, None, ALU.mult).then_inc(neg_made, 1)
                    if due(rear.n):
                        dve.wait_ge(mask_made, rear.n)
                    settle(dve, turns)
                    dve.match_replace(without[:, :], top[:, :], logits[:, :], -3.0e38).then_inc(without_made, 1)
                    dve.wait_ge(without_made, rear.n + 1)
                    if due(rear.n):
                        dve.wait_ge(counted, rear.n)
                    dve.tensor_tensor(mask[:, :], without[:, :], logits[:, :], ALU.not_equal).then_inc(mask_made, 1)
                    if due(16 * K * rear.q):
                        dve.wait_ge(sent[k], 16 * K * rear.q)
                    dve.tensor_scalar(row[k][:, ROW - 1:ROW].bitcast(I32), row[k][:, ROW - 1:ROW].bitcast(I32),
                                      float(2 * P), None, ALU.add).then_inc(row_named, 1)
                    dve.wait_ge(mask_made, rear.n + 1)
                    dve.wait_ge(ex_made, rear.n + 1)
                    if due(rear.n):
                        dve.wait_ge(row_weighted, rear.n)
                    dve.tensor_tensor_reduce(chosen[:, :], ex[:, :], mask[:, :], 1.0, 0.0, ALU.mult, ALU.add,
                                             w_sum[:, :]).then_inc(chosen_made, 1)
                    dve.wait_ge(chosen_made, rear.n + 1)
                    dve.reciprocal(w_inv[:, :], w_sum[:, :]).then_inc(w_inv_made, 1)
                    dve.wait_ge(w_inv_made, rear.n + 1)
                    dve.tensor_scalar(row[k][:, E:E + NX], chosen[:, :], w_inv[:, 0:1], None,
                                      ALU.mult).then_inc(row_weighted, 1)
                    dve.wait_ge(counted, rear.n + 1)
                    if due(rear.n):
                        dve.wait_ge(key_made, rear.n)
                    if due(rear.n):
                        dve.wait_ge(base_moved, rear.n)
                    dve.tensor_tensor(key_free[:, :], key_base[:, :], before_p, ALU.subtract).then_inc(free_made, 1)
                    dve.wait_ge(free_made, rear.n + 1)
                    dve.tensor_tensor(key_base[:, :], key_base[:, :], tile_p, ALU.subtract).then_inc(base_moved, 1)
                    if due(rear.n):
                        dve.wait_ge(key8_made, rear.n)
                    dve.tensor_tensor(key[:, :], key_free[:, :], mask[:, :], ALU.mult).then_inc(key_made, 1)
                    dve.wait_ge(key_made, rear.n + 1)
                    if due(rear.n):
                        dve.wait_ge(slots_made, rear.n)
                    settle(dve, turns)
                    dve.max(key8[:, :], key[:, :]).then_inc(key8_made, 1)
                    dve.wait_ge(key8_made, rear.n + 1)
                    dve.tensor_scalar(slot[k][:, :], key8[:, :], -1.0, float(KEY0), ALU.mult,
                                      ALU.add).then_inc(slots_made, 1)
            run_frames(dve, frame, 2, -1, 2, 30, NT)

            steps = [0]

            def then(ins):
                steps[0] += 1
                ins.then_inc(table_step, 1)
                dve.wait_ge(table_step, steps[0])
            dve.wait_ge(base_moved, NT)
            then(dve.tensor_tensor(count[:, :], cc("key0"), key_base[:, :], ALU.subtract))
            then(dve.tensor_scalar(count[:, :], count[:, :], float(CAP), None, ALU.min))
            wide = [P, NX, CAP // P]
            then(dve.tensor_tensor(count_le[:, :, :], count[:, :].unsqueeze(2).broadcast_to(wide),
                                   cc("steps").unsqueeze(1).broadcast_to(wide), ALU.is_gt))
            then(dve.tensor_reduce(tiles[:, :], count_le[:, :, :], AX.X, ALU.add))
            then(dve.tensor_tensor_scan(tiles_end[:, :], cc("ones")[:, 0:NX], tiles[:, :], 0.0, ALU.mult, ALU.add))
            wide = [P, NCH, NX]
            then(dve.tensor_tensor(past[:, :, :], tiles_end[:, :].unsqueeze(1).broadcast_to(wide),
                                   cc("tile").unsqueeze(2).broadcast_to(wide), ALU.is_le))
            then(dve.tensor_reduce(expert[:, :], past[:, :, :], AX.X, ALU.add))
            then(dve.tensor_tensor(past_tiles[:, :, :], past[:, :, :], tiles[:, :].unsqueeze(1).broadcast_to(wide),
                                   ALU.mult))
            then(dve.tensor_reduce(begun[:, :], past_tiles[:, :, :], AX.X, ALU.add))
            then(dve.tensor_scalar(live[:, :], expert[:, :], float(NX), float(P), ALU.is_lt, ALU.mult))
            then(dve.tensor_tensor(inside[:, :], cc("tile"), begun[:, :], ALU.subtract))
            then(dve.tensor_tensor(inside[:, :], inside[:, :], live[:, :], ALU.mult))
            then(dve.scalar_tensor_tensor(out=values[:, 0, :], in0=expert[:, :], scalar=float(REGION),
                                          in1=inside[:, :], op0=ALU.mult, op1=ALU.add))
            then(dve.tensor_scalar(values[:, 1, :], expert[:, :], float(NX - 1), None, ALU.min))
            dve.tensor_tensor(pad_f[:, :], count[:, :], cc("ebase"), ALU.add).then_inc(values_made, 1)
            dve.wait_ge(values_made, 1)
            dve.tensor_copy(pad_at[:, :], pad_f[0:1, :]).then_inc(tiles_known, 1)
            dve.wait_ge(values_turned, 1)
            dve.tensor_copy(tile_rows[:, :], bank(0, 2)[0:1, 0:2 * NCH * P]).then_inc(tiles_known, 1)
            dve.wait_ge(tiles_known, 2)
            dve.tensor_copy(pad_f[0:1, 0:1], pad_f[0:1, 0:1]).then_inc(routed, 1)

            dve.wait_ge(routed, 2)
            for g in range(NGRP):
                if due(NGRP + g + 1):
                    dve.wait_ge(stage_hi, NGRP + g + 1)
                wide = slice(WG * E * g, WG * E * (g + 1))
                dve.tensor_tensor(w_dn[1][:, wide],
                                  stage[g % 2][0:I, :, :, :].rearrange("i c e w -> i (c e w)")[:, 0:WG * E],
                                  w_dn[0][:, wide].bitcast(F32), ALU.subtract).then_inc(stage_lo, 1)

            def frame_b(s):
                f, h = s.at(1), s.at(-1)
                if f.within(NS):
                    dve.wait_ge(x_hi, f.n + 1)
                    dve.tensor_tensor(x_t[1][f.r % 2][:, :, :, :].rearrange("p i c t -> p (i c t)"), x_t_p[f.r % 2],
                                      x_t[0][f.r % 2][:, :, :, :].rearrange("p i c t -> p (i c t)").bitcast(F32),
                                      ALU.subtract).then_inc(x_lo, 1)
                    dve.wait_ge(rows_in[f.r % 2], 32 * (2 * f.q + f.r // 2 + 1))
                    if due(f.n - 1):
                        dve.wait_ge(inner_made, f.n - 1)
                    for i in range(2):
                        at = dve.value_load(tile_rows[0:1, bass.ds(f.n * 2 + (NCH * P + i), 1)], min_val=0,
                                            max_val=NX - 1)
                        last = dve.tensor_copy(weight[f.r % 2][:, i:i + 1],
                                               rows[f.r % 2][:, i, bass.ds(at + E, 1)])
                    last.then_inc(weight_made, 1)
                    for i in range(2):
                        if due(16 * (2 * f.q + f.r // 2 - 1)):
                            dve.wait_ge(added[(2 * f.r + i) % NACC], 16 * (2 * f.q + f.r // 2 - 1))
                    dve.tensor_copy(tokens[f.r][:, :],
                                    rows[f.r % 2][:, :, ROW - 1].bitcast(U32)).then_inc(tokens_made, 1)
                if s.within(NS):
                    dve.wait_ge(gated_made, s.n + 1)
                    dve.wait_ge(weight_made, s.n + 1)
                    if due(s.n - 1):
                        dve.wait_ge(h_turned, s.n - 1)
                    for i in range(2):
                        last = dve.scalar_tensor_tensor(
                            out=inner[s.r % 2][:, i, :], in0=gated[s.r % 2][:, i, :],
                            scalar=weight[s.r % 2][:, i:i + 1],
                            in1=gu_p[s.r % 2][:, 2 * I * i + I:2 * I * (i + 1)], op0=ALU.mult, op1=ALU.mult)
                    last.then_inc(inner_made, 1)
                if h.within(NS):
                    dve.wait_ge(h_hi, h.n + 1)
                    dve.tensor_tensor(h_t[1][h.r % 2][:, :, :].rearrange("i k t -> i (k t)"), h_t_p[0:I, 0:2 * P],
                                      h_t[0][h.r % 2][:, :, :].rearrange("i k t -> i (k t)").bitcast(F32),
                                      ALU.subtract).then_inc(h_lo, 1)
            run_frames(dve, frame_b, 4, -1, 4, NS - 4, NS)

            for n in range(T // P // CR):
                a = part[n % 2]
                dve.wait_ge(part_in[n % 2], 16 * NACC * (n // 2 + 1))
                dve.tensor_tensor(a[0][:, :], a[0][:, :], a[1][:, :], ALU.add).then_inc(half_sum[0], 1)
                dve.tensor_tensor(a[2][:, :], a[2][:, :], a[3][:, :], ALU.add).then_inc(half_sum[1], 1)
                if due(n + 1):
                    dve.wait_ge(half_sum[0], n + 1)
                if due(n + 1):
                    dve.wait_ge(half_sum[1], n + 1)
                dve.tensor_tensor(a[0][:, :], a[0][:, :], a[2][:, :], ALU.add).then_inc(summed, 1)

        @block.tensor
        def _(pe):
            turns = pe_turns
            pe.wait_ge(consts_in, 32)
            pe.wait_ge(consts_made, 7)

            def frame(t):
                front, rear = t.at(1), t.at(-1)
                k = t.r

                def scores(u):
                    pe.wait_ge(k_masked, t.n + 1)
                    pe.wait_ge(q_copied[u], t.n + 1)
                    if due(t.n):
                        pe.wait_ge(sub_made[u], t.n)
                    for jp in (2 * u, 2 * u + 1):
                        for gp in range(2):
                            for jj in range(2):
                                for b in range(2):
                                    col = (((jp % 2) * 2 + gp) * P) + 512 * jj
                                    r = slice(64 * jj, 64 * jj + 64)
                                    last = pe.matmul(scores_p[u][:, col:col + P],
                                                     q_t[k][r, 2 * jp + gp, S * b:S * b + P],
                                                     k_t[k][r, 2 * jp + b, :, :].rearrange("r g t -> r (g t)"),
                                                     start=(b == 0), stop=(b == 1))
                    last.then_inc(scored[u], 1)

                def turn_sub(u):
                    pe.wait_ge(sub_made[u], t.n + 1)
                    if due(t.n + u):
                        pe.wait_ge(probs_made[1 - u], t.n + u)
                    flat = s_sub[u][:, :, :].rearrange("p x t -> p (x t)")
                    for n in range(8):
                        last = pe.transpose(sub_t_p[:, n * P:(n + 1) * P], flat[:, n * P:(n + 1) * P], ident)
                    last.then_inc(sub_turned[u], 1)

                def attend(u):
                    pe.wait_ge(probs_made[u], t.n + 1)
                    if u == 0:
                        pe.wait_ge(v_copied, t.n + 1)
                        if due(t.n):
                            pe.wait_ge(att_made, t.n)
                    for n in range(8):
                        jj, jp, gp = n // 4, 2 * u + (n // 2) % 2, n % 2
                        j = 4 * jj + jp
                        h = j * G + 2 * gp
                        for b in range(2):
                            last = pe.matmul(out_p[S * b:S * b + S, h:h + 2, :].rearrange("p h c -> p (h c)"),
                                             probs[u][:, n, S * b:S * b + S], v_t[k][:, b, j, :],
                                             start=True, stop=True)
                    last.then_inc(attended[u], 1)

                def turn_q(u):
                    if u == 0:
                        pe.wait_ge(q_lo, front.n + 1)
                        if due(rear.n + 1):
                            pe.wait_ge(logits_copied, rear.n + 1)
                    else:
                        pe.wait_ge(q_copied[0], front.n + 1)
                    for n in range(4):
                        last = pe.transpose(turn_p[:, n * P:(n + 1) * P],
                                            q_parts[:, 4 * u + n, :, :, :].rearrange("t jj p f -> t (jj p f)"), ident)
                    last.then_inc(q_turned[u], 1)

                if t.within(NT):
                    scores(0)
                    scores(1)
                if front.within(NT):
                    pe.wait_ge(k_lo, front.n + 1)
                    if due(front.n):
                        pe.wait_ge(q_copied[1], front.n)
                    if due(rear.n):
                        pe.wait_ge(base_moved, rear.n)
                    for n in range(4):
                        last = pe.transpose(turn_p[:, n * P:(n + 1) * P], 
                                            k_parts[:, n, :, :, :].rearrange("t jj p w -> t (jj p w)"), ident)
                    last.then_inc(k_turned, 1)
                if t.within(NT):
                    turn_sub(0)
                if rear.within(NT):
                    pe.wait_ge(row_normed, rear.n + 1)
                    if front.within(NT):
                        pe.wait_ge(k_masked, front.n + 1)
                    else:
                        if due(rear.n):
                            pe.wait_ge(base_moved, rear.n)
                    for c in range(2):
                        last = pe.transpose(turn_p[:, c * P:(c + 1) * P], row[rear.r][:, c * P:(c + 1) * P], ident)
                    last.then_inc(x2_turned, 1)
                if t.within(NT):
                    attend(0)
                if rear.within(NT):
                    pe.wait_ge(x2_copied, rear.n + 1)
                    for c in range(2):
                        last = pe.matmul(logits_p, x2_t[:, c, :], gw[:, c, :], start=(c == 0), stop=(c == 1))
                    last.then_inc(logits_made, 1)
                if t.within(NT):
                    turn_sub(1)
                if front.within(NT):
                    if not rear.within(NT):
                        pe.wait_ge(k_masked, front.n + 1)
                    turn_q(0)
                if t.within(NT):
                    attend(1)
                if front.within(NT):
                    turn_q(1)
                if rear.within(NT):
                    pe.wait_ge(mask_made, rear.n + 1)
                    if front.within(NT):
                        pe.wait_ge(q_copied[1], front.n + 1)
                    else:
                        pe.wait_ge(logits_copied, rear.n + 1)
                    pe.matmul(before_p, tri_b[:, :], mask[:, :], start=True, stop=True)
                    pe.matmul(tile_p, ones_b[:, :], mask[:, :], start=True, stop=True).then_inc(counted, 1)
            run_frames(pe, frame, 2, -1, 2, 30, NT)

            pe.wait_ge(values_made, 1)
            for v in range(2):
                for c in range(NCH):
                    col = (v * NCH + c) * P
                    last = pe.matmul(bank(0, 2)[0:1, col:col + P], values[:, v, c:c + 1], ident, start=True,
                                     stop=True)
            last.then_inc(values_turned, 1)
            pe.wait_ge(values_turned, 1)
            pe.matmul(bank(2)[0:1, 0:1], values[:, 0, 0:1], ident[:, 0:1], start=True, stop=True).then_inc(routed, 1)
            pe.wait_ge(tiles_known, 2)

            def frame_b(s):
                f, h, b = s.at(1), s.at(-1), s.at(-2)
                if f.within(NS):
                    pe.wait_ge(rows_in[f.r % 2], 32 * (2 * f.q + f.r // 2 + 1))
                    if due(f.n - 1):
                        pe.wait_ge(x_lo, f.n - 1)
                    for i in range(2):
                        for c in range(2):
                            last = pe.transpose(x_t_p[f.r % 2][:, (2 * i + c) * P:(2 * i + c + 1) * P],
                                                rows[f.r % 2][:, i, c * P:(c + 1) * P], ident)
                    last.then_inc(x_turned, 1)
                if s.within(NS):
                    pe.wait_ge(x_lo, s.n + 1)
                    if due(s.n - 1):
                        pe.wait_ge(inner_made, s.n - 1)
                    settle(pe, turns)
                    for i in range(2):
                        at = pe.value_load(tile_rows[0:1, bass.ds(s.n * 2 + (NCH * P + i), 1)], min_val=0,
                                           max_val=NX - 1)
                        todo = [(c, xp, wp) for c in range(2) for xp, wp in ((0, 0), (0, 1), (1, 0))]
                        for n, (c, xp, wp) in enumerate(todo):
                            last = pe.matmul(gu_p[s.r % 2][:, 2 * I * i:2 * I * (i + 1)],
                                             x_t[xp][s.r % 2][:, i, c, :],
                                             w_gu[wp][:, c, bass.ds(at * (2 * I), 2 * I)],
                                             start=(n == 0), stop=(n == len(todo) - 1))
                    last.then_inc(gu_made, 1)
                if h.within(NS):
                    pe.wait_ge(inner_made, h.n + 1)
                    if due(h.n):
                        pe.wait_ge(h_lo, h.n)
                    for i in range(2):
                        last = pe.transpose(h_t_p[0:I, i * P:(i + 1) * P], inner[h.r % 2][:, i, :], ident)
                    last.then_inc(h_turned, 1)
                if b.within(NS):
                    pe.wait_ge(h_lo, b.n + 1)
                    if due(b.n - 1):
                        pe.wait_ge(y_copied, b.n - 1)
                    pe.wait_ge(stage_lo, 2 * NGRP)
                    settle(pe, turns)
                    for i in range(2):
                        at = pe.value_load(tile_rows[0:1, bass.ds(b.n * 2 + (NCH * P + i), 1)], min_val=0,
                                           max_val=NX - 1)
                        todo = ((0, 0), (0, 1), (1, 0))
                        for n, (hp, wp) in enumerate(todo):
                            last = pe.matmul(y_p[b.r % 2][:, i * E:(i + 1) * E], h_t[hp][b.r % 2][:, i, :],
                                             w_dn[wp][:, bass.ds(at * E, E)], start=(n == 0), stop=(n == 2))
                    last.then_inc(y_made, 1)
            run_frames(pe, frame_b, 4, -1, 4, NS - 4, NS + 1)


def kernel(x, ctx_512, L0_ffn_gate_w, L0_ffn_w_gate, L0_ffn_w_up, L0_ffn_w_down):
    import concourse.bacc as bacc
    from concourse.bass_utils import run_bass_kernel_spmd

    arrays = {"x": x, "ctx_in": ctx_512, "gate_w": L0_ffn_gate_w, "w_gate": L0_ffn_w_gate,
              "w_up": L0_ffn_w_up, "w_down": L0_ffn_w_down, "const": constants()}
    arrays = {name: np.ascontiguousarray(a) for name, a in arrays.items()}
    nc = bacc.Bacc("TRN2", target_bir_lowering=False, num_devices=1)
    ins = [nc.dram_tensor(name, a.shape, mybir.dt.from_np(a.dtype), kind="ExternalInput").ap()
           for name, a in arrays.items()]
    out = nc.dram_tensor("out", (B, S, E), F32, kind="ExternalOutput").ap()
    build(nc, *ins, out)
    r = run_bass_kernel_spmd(nc, [arrays], core_ids=[0])
    return r.results[0]["out"]
```

```python
from contextlib import ExitStack

import numpy as np

import concourse.bass as bass
from concourse import mybir

F32 = mybir.dt.float32
F32R = mybir.dt.float32r
BF16 = mybir.dt.bfloat16
I32 = mybir.dt.int32
U32 = mybir.dt.uint32
ALU = mybir.AluOpType
ACT = mybir.ActivationFunctionType
AX = mybir.AxisListType

P = 128
B, S, E = 64, 64, 256
KV, G, D = 8, 4, 8
T = B * S
NT = T // P
NX, K, I = 32, 8, 96
CAP = 2 * (T * K // NX)
REGION = T + P
NULL = NX * REGION
ROW = E + NX + 1
NB = -(-(T * K // P + NX) // 8) * 8
NS = NB // 2
KEY0 = 1 << 18
EPS = 1e-5
SCALE = float(D) ** -0.5
NACC = 4
VC = D + 1
WG = 4

CONST_COLS = {}
_at = 0
for _name, _width in (("ident", P), ("tri", P), ("gmask", 2), ("ebase", NX), ("key0", NX), ("tok", 2), ("pad", 1),
                      ("tile", NB // P + 1), ("steps", CAP // P), ("number", NX), ("ones", P)):
    CONST_COLS[_name] = slice(_at, _at + _width)
    _at += _width
NCONST = _at
NCH = NB // P + 1


def constants():
    c = np.zeros((P, NCONST), np.float32)
    p = np.arange(P)[:, None]
    c[:, CONST_COLS["ident"]] = p == np.arange(P)
    c[:, CONST_COLS["tri"]] = p < np.arange(P)
    c[:, CONST_COLS["gmask"]] = (p % 16) // 8 == np.arange(2)
    c[:, CONST_COLS["ebase"]] = np.arange(NX) * REGION
    c[:, CONST_COLS["key0"]] = KEY0 - np.arange(NX) * REGION
    c[:, CONST_COLS["tok"]] = p + P * np.arange(2) - 2 * P
    c[:, CONST_COLS["pad"]] = T + p
    c[:, CONST_COLS["tile"]] = p + P * np.arange(NCH)
    c[:, CONST_COLS["steps"]] = P * np.arange(CAP // P)
    c[:, CONST_COLS["number"]] = np.arange(NX)
    c[:, CONST_COLS["ones"]] = 1.0
    return c


class Step:

    def __init__(self, q, r, ring):
        self.q, self.r, self.ring = q, r, ring

    def at(self, d):
        return Step(self.q + (self.r + d) // self.ring, (self.r + d) % self.ring, self.ring)

    @property
    def n(self):
        return self.q * self.ring + self.r

    def within(self, count):
        return not isinstance(self.q, int) or 0 <= self.n < count


def run_frames(eng, frame, ring, first, loop_from, loop_to, last):
    for n in range(first, loop_from):
        frame(Step(n // ring, n % ring, ring))
    with eng.Fori(loop_from // ring, loop_to // ring) as i:
        for k in range(ring):
            frame(Step(i, k, ring))
    for n in range(loop_to, last + 1):
        frame(Step(n // ring, n % ring, ring))


def due(value):
    return not isinstance(value, int) or value > 0


def at_most(value, most):
    return min(value, most) if isinstance(value, int) else value


def load_values(nc, engine, values, most):
    _, registers = nc.values_load_multi_w_load_instructions(
        values, engines=(engine,), min_val=0, max_val=most,
        skip_runtime_bounds_check_because="they are clamped as they are computed")
    return registers


def settle(eng, turns):
    eng.sem_inc(turns, 1)


def build(nc, x, ctx_in, gate_w, w_gate, w_up, w_down, const, out):
    xf = x.rearrange("b s e -> (b s) e")
    cf = ctx_in.rearrange("b s e -> (b s) e")
    outf = out.rearrange("b s e -> (b s) e")
    table = nc.dram_tensor("table", (NULL + P, ROW), F32, kind="Internal").ap()
    acc = [nc.dram_tensor(f"acc{i}", (T + P, E), F32, kind="Internal").ap() for i in range(NACC)]

    with ExitStack() as stack:
        def sem(name):
            return stack.enter_context(nc.semaphore(name))

        def sems(name, n):
            return [sem(f"{name}{i}") for i in range(n)]

        def allocate(where):
            def sb(name, shape, dt=F32):
                return where.enter_context(nc.sbuf_tensor(name, shape, dt))
            return sb

        sb = allocate(stack)
        con = sb("con", [P, NCONST])
        tri_b = sb("tri_b", [P, P], BF16)
        ones_b = sb("ones_b", [P, P], BF16)
        gw = sb("gw", [P, 2, NX])
        pad_row = sb("pad_row", [P, ROW])
        key_base = sb("key_base", [P, NX])
        w_gu = [sb(f"w_gu_{x}", [P, 2, NX * 2 * I], F32R) for x in ("hi", "lo")]
        tile_rows = sb("tile_rows", [1, NCH * P], I32)
        tile_experts = sb("tile_experts", [1, 4 + NCH * P], I32)
        expert_of = sb("expert_of", [P, NCH * P])
        pad_at = sb("pad_at", [1, NX], I32)

        def cc(name):
            return con[:, CONST_COLS[name]]
        ident = cc("ident")

        phase_a = ExitStack()
        sb = allocate(phase_a)
        stage = [sb(f"stage{i}", [P, 2, 2 * I]) for i in range(2)]
        x_q = [sb(f"x_q{i}", [P, E]) for i in range(2)]
        x_r = [sb(f"x_r{i}", [P, E]) for i in range(2)]
        ctx_t = [sb(f"ctx_t{i}", [P, KV * D]) for i in range(2)]
        ctx_v = [sb(f"ctx_v{i}", [P, 2, KV * D]) for i in range(2)]
        q_n = sb("q_n", [P, E])
        q_parts = sb("q_parts", [P, 8, 2, 4, 16])
        k_parts = sb("k_parts", [P, 4, 2, 2, 4 * D])
        q_t = [sb(f"q_t{i}", [P, 8, 3 * S], F32R) for i in range(2)]
        k_t = [sb(f"k_t{i}", [P, 8, 2, S], F32R) for i in range(2)]
        v_t = [sb(f"v_t{i}", [P, 2, KV, 2 * VC]) for i in range(2)]
        s_max = [sb(f"s_max{i}", [P, 16]) for i in range(2)]
        s_sub = [sb(f"s_sub{i}", [P, 16, S]) for i in range(2)]
        probs = [sb(f"probs{i}", [P, 8, P]) for i in range(2)]
        inv = sb("inv", [P, KV * G])
        att = sb("att", [P, E])
        x1 = [sb(f"x1_{i}", [P, E]) for i in range(2)]
        stats = sb("stats", [P, 2, 6])
        mean_var = sb("mean_var", [P, 2, 2])
        var_eps = sb("var_eps", [P, 2])
        half = sb("half", [P, 2])
        rstd = sb("rstd", [P, 2])
        shift = sb("shift", [P, 2])
        row = [sb(f"row{i}", [P, ROW]) for i in range(2)]
        x2_t = sb("x2_t", [P, 2, P])
        top = sb("top", [P, 8])
        neg_top = sb("neg_top", [P, 1])
        logits = sb("logits", [P, NX])
        ex = sb("ex", [P, NX])
        without = sb("without", [P, NX])
        mask = sb("mask", [P, NX], BF16)
        chosen = sb("chosen", [P, NX])
        w_sum = sb("w_sum", [P, 1])
        w_inv = sb("w_inv", [P, 1])
        key_free = sb("key_free", [P, NX])
        key = sb("key", [P, NX])
        key8 = sb("key8", [P, 8])
        slot = [sb(f"slot{i}", [P, 8], U32) for i in range(2)]
        zeros = sb("zeros", [P, E])
        count = sb("count", [P, NX])
        count_le = sb("count_le", [P, NX, CAP // P])
        tiles = sb("tiles", [P, NX])
        tiles_end = sb("tiles_end", [P, NX])
        past = sb("past", [P, NCH, NX])
        past_tiles = sb("past_tiles", [P, NCH, NX])
        expert = sb("expert", [P, NCH])
        begun = sb("begun", [P, NCH])
        live = sb("live", [P, NCH])
        inside = sb("inside", [P, NCH])
        values = sb("values", [P, 2, NCH])
        pad_f = sb("pad_f", [P, NX])
        phase_a.close()

        phase_b = ExitStack()
        sb = allocate(phase_b)
        w_dn = [sb(f"w_dn_{x}", [I, NX * E], F32R) for x in ("hi", "lo")]
        rows = [sb(f"rows{i}", [P, 2, ROW]) for i in range(4)]
        x_t = [[sb(f"x_t_{x}{i}", [P, 2, 2, P], F32R) for i in range(2)] for x in ("hi", "lo")]
        gated = [sb(f"gated{i}", [P, 2, I]) for i in range(2)]
        inner = [sb(f"inner{i}", [P, 2, I]) for i in range(2)]
        h_t = [[sb(f"h_t_{x}{i}", [I, 2, P], F32R) for i in range(2)] for x in ("hi", "lo")]
        y = [sb(f"y{i}", [P, 2, E]) for i in range(4)]
        weight = [sb(f"weight{i}", [P, 2]) for i in range(2)]
        weights = [sb(f"weights{i}", [P, 2, NX]) for i in range(2)]
        tokens = sb("tokens", [P, 2 * NS], U32)
        targets = [sb(f"targets{i}", [P, 2], U32) for i in range(4)]
        phase_b.close()
        phase_c = ExitStack()
        sb = allocate(phase_c)
        CR = 4
        part = [[sb(f"part{i}_{a}", [P, CR * E]) for a in range(NACC)] for i in range(2)]
        phase_c.close()

        psum = stack.enter_context(nc.psum_tensor("psum", [P, 8, 512], F32))

        def bank(n, k=1):
            return psum[:, n:n + k, :].rearrange("p k c -> p (k c)")
        scores_p = [bank(0, 2), bank(2, 2)]
        k_turn_p = bank(4)
        q_turn_p = [bank(5), bank(4)]
        route_p = bank(6)
        out_p = bank(7)[:, 0:KV * G * VC].rearrange("p (h c) -> p h c", c=VC)
        logits_p = route_p[:, 0:NX]
        before_p = route_p[:, 0:NX]
        tile_p = route_p[:, NX:2 * NX]
        x_t_p = [bank(0), bank(1)]
        gu_p = [bank(2), bank(3)]
        h_t_p = [bank(4), bank(7)]
        y_p = [bank(5), bank(6)]

        def key_view(jj, low):
            return k_parts[:, :, jj, low, :].rearrange("t jp (x d) -> t jp x d", d=D)

        def key_source(k, jj):
            return (ctx_t[k][:, 32 * jj:32 * jj + 32].rearrange("t (jp d) -> t jp d", d=D).unsqueeze(2)
                    .broadcast_to([P, 4, 4, D]))

        def query_source(jj):
            return (q_n[:, P * jj:P * jj + P].rearrange("t (n f) -> t n f", f=16).unsqueeze(2)
                    .broadcast_to([P, 8, 2, 16]))

        pool_turns = sem("pool_turns")
        dve_turns = sem("dve_turns")
        pe_turns = sem("pe_turns")
        act_turns = sem("act_turns")
        consts_in = sem("consts_in")
        consts_made = sem("consts_made")
        ones_made = sem("ones_made")
        pool_ready = sem("pool_ready")
        stage_in = sems("stage_in", 2)
        gu_hi = sem("gu_hi")
        gu_lo = sem("gu_lo")
        down_in = sems("down_in", NX // WG)
        down_hi = sem("down_hi")
        down_lo = sem("down_lo")
        x_q_in = sems("x_q_in", 2)
        x_r_in = sems("x_r_in", 2)
        ctx_in_s = sems("ctx_in_s", 2)
        ctx_v_in = sems("ctx_v_in", 2)
        x1_out = sems("x1_out", 2)
        zero_out = sem("zero_out")
        null_out = sem("null_out")
        k_hi = sem("k_hi")
        k_lo = sem("k_lo")
        k_turned = sem("k_turned")
        k_masked = sem("k_masked")
        v_copied = sem("v_copied")
        scored = sems("scored", 2)
        max_made = sems("max_made", 2)
        sub_made = sems("sub_made", 2)
        sub_turned = sems("sub_turned", 2)
        probs_made = sems("probs_made", 2)
        attended = sems("attended", 2)
        stats1 = sem("stats1")
        stats2 = sem("stats2")
        aggr1 = sem("aggr1")
        aggr2 = sem("aggr2")
        var_made = sem("var_made")
        rstd_made = sem("rstd_made")
        shift_made = sem("shift_made")
        inv_made = sem("inv_made")
        att_made = sem("att_made")
        x1_made = sem("x1_made")
        q_normed = sem("q_normed")
        q_hi = sem("q_hi")
        q_lo = sem("q_lo")
        q_turned = sems("q_turned", 2)
        q_copied = sems("q_copied", 2)
        row_normed = sem("row_normed")
        row_weighted = sem("row_weighted")
        row_named = sem("row_named")
        x2_turned = sem("x2_turned")
        x2_copied = sem("x2_copied")
        logits_made = sem("logits_made")
        logits_copied = sem("logits_copied")
        top_made = sem("top_made")
        neg_made = sem("neg_made")
        ex_made = sem("ex_made")
        without_made = sem("without_made")
        mask_made = sem("mask_made")
        chosen_made = sem("chosen_made")
        w_inv_made = sem("w_inv_made")
        counted = sem("counted")
        free_made = sem("free_made")
        key_made = sem("key_made")
        base_moved = sem("base_moved")
        key8_made = sem("key8_made")
        slots_made = sem("slots_made")
        sent = sems("sent", 2)
        routed = sem("routed")
        table_step = sem("table_step")
        values_made = sem("values_made")
        values_turned = sem("values_turned")
        tiles_known = sem("tiles_known")
        pads_out = sem("pads_out")

        rows_in = sems("rows_in", 4)
        x_turned = sem("x_turned")
        x_hi = sem("x_hi")
        x_lo = sem("x_lo")
        weight_made = sem("weight_made")
        weights_made = sem("weights_made")
        tokens_made = sem("tokens_made")
        targets_made = sem("targets_made")
        gu_made = sem("gu_made")
        gated_made = sem("gated_made")
        inner_made = sem("inner_made")
        h_turned = sem("h_turned")
        h_hi = sem("h_hi")
        h_lo = sem("h_lo")
        y_made = sem("y_made")
        y_copied = sem("y_copied")
        added = sems("added", NACC)
        part_in = sems("part_in", 2)
        half_sum = sems("half_sum", 2)
        summed = sem("summed")
        out_done = sems("out_done", 2)

        NGRP = NX // WG
        ZEROS = (NACC - 1) * NT + NACC
        assert NX == NT and KV * D == 64
        block = stack.enter_context(nc.Block())

        @block.sync
        def _(sp):
            sp.dma_start(con[:, :], const).then_inc(consts_in, 16)
            sp.dma_start(gw[:, :, :], gate_w.rearrange("(c p) e -> p c e", p=P)).then_inc(consts_in, 16)

            def load_weights(e):
                if due(e.n - 1):
                    sp.wait_ge(gu_lo, e.n - 1)
                for m, w in enumerate((w_gate, w_up)):
                    sp.dma_start(stage[e.r][:, :, I * m:I * (m + 1)],
                                 w[bass.ds(e.n, 1), :, :].rearrange("o (c p) i -> p (o c) i", p=P)
                                 ).then_inc(stage_in[e.r], 16)

            def load_front(t):
                k = t.r
                if due(t.n - 1):
                    sp.wait_ge(q_normed, t.n - 1)
                sp.dma_start(x_q[k][:, :], xf[bass.ds(t.n * P, P), :]).then_inc(x_q_in[k], 16)
                if due(t.n - 1):
                    sp.wait_ge(k_lo, t.n - 1)
                sp.dma_start(ctx_t[k][:, :], cf[bass.ds(t.n * P, P), :]).then_inc(ctx_in_s[k], 16)

            def load_values_of(t):
                k = t.r
                if due(t.n - 1):
                    sp.wait_ge(v_copied, t.n - 1)
                for g in range(2):
                    sp.dma_start(ctx_v[k][S * g:S * g + S, :, :],
                                 cf[bass.ds(t.n * P, P), :].rearrange("(b t) f -> t b f", b=2)
                                 ).then_inc(ctx_v_in[k], 16)

            def frame(t):
                if t.at(3).within(NT):
                    load_front(t.at(3))
                if t.at(2).within(NT):
                    load_values_of(t.at(2))
                if t.at(1).within(NX):
                    load_weights(t.at(1))
                if t.within(NT):
                    if due(t.n - 1):
                        sp.wait_ge(x1_made, t.n - 1)
                    sp.dma_start(x_r[t.r][:, :], xf[bass.ds(t.n * P, P), :]).then_inc(x_r_in[t.r], 16)
                    for a in range(1, NACC):
                        sp.dma_start(acc[a][bass.ds(t.n * P, P), :], zeros[:, :]).then_inc(zero_out, 16)
                if t.at(-1).within(NT):
                    u = t.at(-1)
                    sp.wait_ge(x1_made, u.n + 1)
                    sp.dma_start(acc[0][bass.ds(u.n * P, P), :], x1[u.r][:, :]).then_inc(x1_out[u.r], 16)

            frame(Step(-2, 1, 2))
            frame(Step(-1, 0, 2))
            frame(Step(-1, 1, 2))
            sp.wait_ge(pool_ready, 3)
            for a in range(NACC):
                sp.dma_start(acc[a][T:T + P, :], zeros[:, :]).then_inc(zero_out, 16)
            sp.dma_start(table[NULL:NULL + P, :], pad_row[:, :]).then_inc(null_out, 16)
            run_frames(sp, frame, 2, 0, 2, 28, NT)

            for k in range(2):
                sp.wait_ge(sent[k], 16 * K * (NT // 2))
                sp.wait_ge(x1_out[k], 16 * (NT // 2))
            sp.wait_ge(tiles_known, 4)
            with sp.Fori(0, NX // 8) as e:
                ats = load_values(nc, mybir.EngineType.SP, pad_at[0:1, bass.ds(e * 8, 8)], NULL - P)
                for at in ats:
                    sp.dma_start(table[bass.ds(at, P), :], pad_row[:, :]).then_inc(pads_out, 16)
            sp.wait_ge(pads_out, 16 * NX)
            sp.wait_ge(null_out, 16)
            sp.wait_ge(routed, 2)

            at = []

            def load_rows(s):
                if s.r == 0:
                    at[:] = load_values(nc, mybir.EngineType.SP, tile_rows[0:1, bass.ds(s.n * 2, 8)], NULL)
                if due(s.n - 3):
                    sp.wait_ge(x_turned, s.n - 3)
                if due(s.n - 3):
                    sp.wait_ge(tokens_made, s.n - 3)
                for i in range(2):
                    sp.dma_start(rows[s.r][:, i, :], table[bass.ds(at[2 * s.r + i], P), :]).then_inc(rows_in[s.r], 16)

            run_frames(sp, load_rows, 4, 0, 4, NS, NS - 1)

            for a in range(NACC):
                sp.wait_ge(added[a], 16 * NB // NACC)
            sp.wait_ge(zero_out, 16 * ZEROS)
            chunks = [[a_[0:T, :].rearrange("(p r) e -> p (r e)", p=P)[:, n * CR * E:(n + 1) * CR * E] for a_ in acc]
                      for n in range(T // P // CR)]
            final = [outf.rearrange("(p r) e -> p (r e)", p=P)[:, n * CR * E:(n + 1) * CR * E]
                     for n in range(T // P // CR)]
            for n in range(len(chunks) + 1):
                if n < len(chunks):
                    if due(16 * (n // 2)):
                        sp.wait_ge(out_done[n % 2], 16 * (n // 2))
                    for a in range(NACC):
                        sp.dma_start(part[n % 2][a][:, :], chunks[n][a]).then_inc(part_in[n % 2], 16)
                if n >= 1:
                    if due(n):
                        sp.wait_ge(summed, n)
                    sp.dma_start(final[n - 1], part[(n - 1) % 2][0][:, :]).then_inc(out_done[(n - 1) % 2], 16)
            for k in range(2):
                sp.wait_ge(out_done[k], 16 * len(chunks) // 2)

        @block.gpsimd
        def _(pool):
            turns = pool_turns
            pool.memset(zeros[:, :], 0.0).then_inc(pool_ready, 1)
            pool.memset(half[:, :], -0.5).then_inc(pool_ready, 1)
            pool.wait_ge(consts_made, 8)
            pool.memset(pad_row[:, 0:ROW - 1], 0.0).then_inc(pool_ready, 1)
            pool.wait_ge(pool_ready, 3)

            def frame(t):
                def send(u, first, last):
                    for k in range(first, last):
                        pool.indirect_dma_start(out=table[:, :],
                                                out_offset=bass.IndirectOffsetOnAxis(ap=slot[u.r][:, k:k + 1], axis=0),
                                                in_=row[u.r][:, :], in_offset=None).then_inc(sent[u.r], 16)
                if t.at(-2).within(NT):
                    u = t.at(-2)
                    pool.wait_ge(slots_made, u.n + 1)
                    pool.wait_ge(row_weighted, u.n + 1)
                    pool.wait_ge(row_named, u.n + 1)
                    pool.wait_ge(row_normed, u.n + 1)
                    settle(pool, turns)
                    send(u, 0, K // 2)
                lo = 0 if t.at(-1).within(NT) else 1
                hi = 2 if t.at(2).within(NT) else 1
                if lo < hi:
                    pool.wait_ge(var_made, t.n + 3)
                    if due(t.n + 2):
                        pool.wait_ge(shift_made, t.n + 2)
                    if due(t.n - 1):
                        pool.wait_ge(row_normed, t.n - 1)
                    if due(at_most(t.n + 2, NT)):
                        pool.wait_ge(q_normed, at_most(t.n + 2, NT))
                    pool.tensor_tensor(rstd[:, lo:hi], var_eps[:, lo:hi], half[:, lo:hi],
                                       ALU.pow).then_inc(rstd_made, 1)
                if t.at(-2).within(NT):
                    send(t.at(-2), K // 2, K)
            run_frames(pool, frame, 2, -2, 2, 30, NT + 1)

            pool.wait_ge(zero_out, 16 * ZEROS)
            for k in range(2):
                pool.wait_ge(x1_out[k], 16 * (NT // 2))

            def add(s):
                for i in range(2):
                    a = (2 * s.r + i) % NACC
                    if due(16 * (s.q * 2 + s.r // 2)):
                        pool.wait_ge(added[a], 16 * (s.q * 2 + s.r // 2))
                    pool.wait_ge(y_copied, s.n + 1)
                    pool.wait_ge(targets_made, s.n + 1)
                    settle(pool, turns)
                    pool.indirect_dma_start(out=acc[a][:, :],
                                            out_offset=bass.IndirectOffsetOnAxis(ap=targets[s.r][:, i:i + 1], axis=0),
                                            in_=y[s.r][:, i, :], in_offset=None,
                                            compute_op=ALU.add).then_inc(added[a], 16)
            run_frames(pool, add, 4, 0, 4, NS, NS - 1)

        @block.scalar
        def _(act):
            turns = act_turns
            act.wait_ge(consts_in, 32)
            act.wait_ge(ones_made, 6)

            def frame(t):
                front, rear = t.at(2), t.at(-1)
                if front.within(NT):
                    k = front.r
                    act.wait_ge(ctx_in_s[k], 16 * (front.q + 1))
                    if due(front.n):
                        act.wait_ge(k_turned, front.n)
                    for jj in range(2):
                        last = act.copy(key_view(jj, 0).bitcast(F32R), key_source(k, jj))
                    last.then_inc(k_hi, 1)
                if t.within(NX):
                    act.wait_ge(stage_in[t.r], 32 * (t.q + 1))
                    settle(act, turns)
                    act.copy(w_gu[0][:, :, bass.ds(t.n * (2 * I), 2 * I)], stage[t.r][:, :, :]).then_inc(gu_hi, 1)
                if t.at(1).within(NT):
                    n = t.at(1)
                    act.wait_ge(ctx_v_in[n.r], 32 * (n.q + 1))
                    for u in range(2):
                        if due(n.n - 1):
                            act.wait_ge(attended[u], n.n - 1)
                    for g in range(2):
                        half_p = slice(S * g, S * g + S)
                        last = act.copy(v_t[n.r][half_p, :, :, VC * g:VC * g + D].rearrange("t b j d -> t (b j) d"),
                                        ctx_v[n.r][half_p, :, :].rearrange("t b (j d) -> t (b j) d", d=D))
                    last.then_inc(v_copied, 1)

                def probabilities(u):
                    act.wait_ge(sub_turned[u], t.n + 1)
                    if due(t.n):
                        act.wait_ge(attended[u], t.n)
                    act.activation(probs[u][:, :, :].rearrange("p x s -> p (x s)"), scores_p[u],
                                   ACT.Exp, scale=SCALE).then_inc(probs_made[u], 1)
                if t.within(NT):
                    probabilities(0)
                if rear.within(NT):
                    k = rear.r
                    act.wait_ge(shift_made, t.n + 3)
                    if due(16 * K * rear.q):
                        act.wait_ge(sent[k], 16 * K * rear.q)
                    act.activation(row[k][:, 0:E], x1[k][:, :], ACT.Identity, bias=shift[:, 0:1],
                                   scale=rstd[:, 0:1]).then_inc(row_normed, 1)
                if front.within(NT):
                    k = front.r
                    act.wait_ge(shift_made, t.n + 3)
                    if due(front.n):
                        act.wait_ge(q_lo, front.n)
                    act.activation(q_n[:, :], x_q[k][:, :], ACT.Identity, bias=shift[:, 1:2],
                                   scale=rstd[:, 1:2]).then_inc(q_normed, 1)
                    act.wait_ge(q_normed, front.n + 1)
                    for u in range(2):
                        if due(front.n):
                            act.wait_ge(q_turned[u], front.n)
                    for jj in range(2):
                        last = act.copy(q_parts[:, :, jj, 0:4:2, :].bitcast(F32R), query_source(jj))
                    last.then_inc(q_hi, 1)
                if rear.within(NT):
                    act.wait_ge(x2_turned, rear.n + 1)
                    if due(rear.n):
                        act.wait_ge(logits_made, rear.n)
                    act.copy(x2_t[:, :, :].rearrange("p c t -> p (c t)"), route_p[:, 0:E]).then_inc(x2_copied, 1)
                if front.within(NT):
                    k = front.r
                    act.wait_ge(k_turned, front.n + 1)
                    for u in range(2):
                        if due(front.n - 1):
                            act.wait_ge(scored[u], front.n - 1)
                    for g in range(2):
                        last = act.activation(k_t[k][:, :, g, :], k_turn_p.rearrange("r (x t) -> r x t", t=S),
                                              ACT.Copy, scale=cc("gmask")[:, g:g + 1])
                    last.then_inc(k_masked, 1)
                if rear.within(NT):
                    act.wait_ge(neg_made, rear.n + 1)
                    if due(rear.n):
                        act.wait_ge(chosen_made, rear.n)
                    act.activation(ex[:, :], logits[:, :], ACT.Exp, bias=neg_top[:, 0:1]).then_inc(ex_made, 1)
                if t.within(NT):
                    probabilities(1)
                if front.within(NT):
                    for u in range(2):
                        act.wait_ge(q_turned[u], front.n + 1)
                        if due(front.n - 1):
                            act.wait_ge(scored[u], front.n - 1)
                        src = q_turn_p[u].rearrange("r (c b s) -> r c b s", b=2, s=S)
                        dst = q_t[front.r][:, 4 * u:4 * u + 4, :].rearrange("r c (b s) -> r c b s", b=3)[:, :, 0:3:2, :]
                        act.copy(dst, src).then_inc(q_copied[u], 1)

            run_frames(act, frame, 2, -2, 2, 30, NT)

            act.wait_ge(routed, 2)
            for k in range(2):
                act.wait_ge(sent[k], 16 * K * (NT // 2))
                act.wait_ge(x1_out[k], 16 * (NT // 2))
            act.wait_ge(zero_out, 16 * ZEROS)
            for g in range(NGRP):
                wide = slice(WG * E * g, WG * E * (g + 1))
                act.dma_start(w_dn[1][:, wide].bitcast(F32).rearrange("i (e h) -> i e h", h=E),
                              w_down[WG * g:WG * g + WG, :, :].rearrange("e i h -> i e h")).then_inc(down_in[g], 16)
            for g in range(NGRP):
                wide = slice(WG * E * g, WG * E * (g + 1))
                act.wait_ge(down_in[g], 16)
                act.copy(w_dn[0][:, wide], w_dn[1][:, wide].bitcast(F32)).then_inc(down_hi, 1)

            def frame_b(s):
                f, h, b = s.at(1), s.at(-1), s.at(-2)
                if f.within(NS):
                    act.wait_ge(x_turned, f.n + 1)
                    if due(f.n - 1):
                        act.wait_ge(gu_made, f.n - 1)
                    act.copy(x_t[0][f.r % 2][:, :, :, :].rearrange("p i c t -> p (i c t)"),
                             x_t_p[f.r % 2]).then_inc(x_hi, 1)
                if s.within(NS):
                    act.wait_ge(gu_made, s.n + 1)
                    if due(s.n - 1):
                        act.wait_ge(inner_made, s.n - 1)
                    act.activation(gated[s.r % 2][:, :, :],
                                   gu_p[s.r % 2][:, 0:4 * I].rearrange("p (i w) -> p i w", i=2)[:, :, 0:I],
                                   ACT.Silu).then_inc(gated_made, 1)
                if b.within(NS):
                    act.wait_ge(y_made, b.n + 1)
                    for i in range(2):
                        if due(16 * (b.q * 2 + b.r // 2 - 1)):
                            act.wait_ge(added[(2 * b.r + i) % NACC], 16 * (b.q * 2 + b.r // 2 - 1))
                    act.copy(y[b.r][:, :, :].rearrange("p i e -> p (i e)"), y_p[b.r % 2]).then_inc(y_copied, 1)
                if h.within(NS):
                    act.wait_ge(h_turned, h.n + 1)
                    if due(h.n - 1):
                        act.wait_ge(y_made, h.n - 1)
                    act.copy(h_t[0][h.r % 2][:, :, :].rearrange("i k t -> i (k t)"),
                             h_t_p[h.r % 2][0:I, 0:2 * P]).then_inc(h_hi, 1)
            run_frames(act, frame_b, 4, -1, 4, NS - 4, NS + 1)

        @block.vector
        def _(dve):
            turns = dve_turns
            dve.wait_ge(consts_in, 32)
            dve.tensor_copy(tri_b[:, :], cc("tri")).then_inc(consts_made, 1)
            dve.tensor_copy(ones_b[:, :], cc("ones")).then_inc(consts_made, 1)
            dve.tensor_copy(key_base[:, :], cc("key0")).then_inc(consts_made, 1)
            dve.tensor_copy(pad_row[:, ROW - 1:ROW].bitcast(U32), cc("pad")).then_inc(consts_made, 1)
            for k in range(2):
                dve.tensor_copy(row[k][:, ROW - 1:ROW].bitcast(I32), cc("tok")[:, k:k + 1]).then_inc(consts_made, 1)
            dve.memset(stats[:, :, :], 0.0).then_inc(consts_made, 1)
            for k in range(2):
                if k == 0:
                    dve.memset(tile_experts[:, 0:4], 0).then_inc(consts_made, 1)
                dve.memset(q_t[k][:, :, S:2 * S].bitcast(F32), 0.0).then_inc(ones_made, 1)
                dve.memset(v_t[k][:, :, :, :], 0.0).then_inc(ones_made, 1)
            dve.wait_ge(ones_made, 4)
            for k in range(2):
                for g in range(2):
                    last = dve.memset(v_t[k][S * g:S * g + S, :, :, VC * g + D:VC * g + VC], 1.0)
                last.then_inc(ones_made, 1)
            def frame(t):
                front, rear = t.at(2), t.at(-1)

                def unit_max(u):
                    dve.wait_ge(scored[u], t.n + 1)
                    if due(t.n):
                        dve.wait_ge(sub_made[u], t.n)
                    dve.tensor_reduce(s_max[u][:, :], scores_p[u].rearrange("p (x t) -> p x t", t=S),
                                      AX.X, ALU.max).then_inc(max_made[u], 1)

                def unit_sub(u):
                    dve.wait_ge(max_made[u], t.n + 1)
                    if due(t.n):
                        dve.wait_ge(sub_turned[u], t.n)
                    dve.tensor_tensor(s_sub[u][:, :, :], scores_p[u].rearrange("p (x t) -> p x t", t=S),
                                      s_max[u][:, :].unsqueeze(2).broadcast_to([P, 16, S]),
                                      ALU.subtract).then_inc(sub_made[u], 1)
                if t.within(NT):
                    unit_max(0)
                    unit_sub(0)
                lo = 0 if rear.within(NT) else 1
                hi = 2 if front.within(NT) else 1
                if front.within(NT):
                    k = front.r
                    dve.wait_ge(x_q_in[k], 16 * (front.q + 1))
                    if due(front.n):
                        dve.wait_ge(aggr1, front.n)
                    dve.bn_stats(stats[:, 1, :], x_q[k][:, :]).then_inc(stats1, 1)
                if rear.within(NT):
                    k = rear.r
                    for u in range(2):
                        dve.wait_ge(attended[u], rear.n + 1)
                    if due(rear.n):
                        dve.wait_ge(att_made, rear.n)
                    dve.reciprocal(inv[:, :], out_p[:, :, D]).then_inc(inv_made, 1)
                    dve.wait_ge(inv_made, rear.n + 1)
                    if due(rear.n):
                        dve.wait_ge(x1_made, rear.n)
                    dve.tensor_tensor(att[:, :].rearrange("p (h d) -> p h d", d=D), out_p[:, :, 0:D],
                                      inv[:, :].unsqueeze(2).broadcast_to([P, KV * G, D]),
                                      ALU.mult).then_inc(att_made, 1)
                    dve.wait_ge(att_made, rear.n + 1)
                    dve.wait_ge(x_r_in[k], 16 * (rear.q + 1))
                    if due(16 * rear.q):
                        dve.wait_ge(x1_out[k], 16 * rear.q)
                    if due(rear.n - 1):
                        dve.wait_ge(row_normed, rear.n - 1)
                    dve.tensor_tensor(x1[k][:, :], att[:, :], x_r[k][:, :], ALU.add).then_inc(x1_made, 1)
                if front.within(NT):
                    dve.wait_ge(stats1, front.n + 1)
                    if due(t.n + 2):
                        dve.wait_ge(shift_made, t.n + 2)
                    settle(dve, turns)
                    dve.bn_aggr(mean_var[:, 1, :], stats[:, 1, :]).then_inc(aggr1, 1)
                if rear.within(NT):
                    dve.wait_ge(x1_made, rear.n + 1)
                    if due(rear.n):
                        dve.wait_ge(aggr2, rear.n)
                    dve.bn_stats(stats[:, 0, :], x1[rear.r][:, :]).then_inc(stats2, 1)
                    dve.wait_ge(stats2, rear.n + 1)
                    if due(t.n + 2):
                        dve.wait_ge(shift_made, t.n + 2)
                    settle(dve, turns)
                    dve.bn_aggr(mean_var[:, 0, :], stats[:, 0, :]).then_inc(aggr2, 1)
                    dve.wait_ge(aggr2, rear.n + 1)
                if lo < hi:
                    if front.within(NT):
                        dve.wait_ge(aggr1, front.n + 1)
                    if due(t.n + 2):
                        dve.wait_ge(rstd_made, t.n + 2)
                    dve.tensor_scalar(var_eps[:, lo:hi], mean_var[:, lo:hi, 1], EPS, None,
                                      ALU.add).then_inc(var_made, 1)
                if front.within(NT):
                    dve.wait_ge(k_hi, front.n + 1)
                    for jj in range(2):
                        last = dve.tensor_tensor(key_view(jj, 1).bitcast(F32R), key_source(front.r, jj),
                                                 key_view(jj, 0), ALU.subtract)
                    last.then_inc(k_lo, 1)
                if t.within(NX):
                    dve.wait_ge(gu_hi, t.n + 1)
                    settle(dve, turns)
                    wide = bass.ds(t.n * (2 * I), 2 * I)
                    dve.tensor_tensor(w_gu[1][:, :, wide], stage[t.r][:, :, :], w_gu[0][:, :, wide].bitcast(F32),
                                      ALU.subtract).then_inc(gu_lo, 1)
                if lo < hi:
                    dve.wait_ge(rstd_made, t.n + 3)
                    if due(rear.n):
                        dve.wait_ge(row_normed, rear.n)
                    if due(at_most(t.n + 2, NT)):
                        dve.wait_ge(q_normed, at_most(t.n + 2, NT))
                    dve.scalar_tensor_tensor(out=shift[:, lo:hi], in0=mean_var[:, lo:hi, 0], scalar=-1.0,
                                             in1=rstd[:, lo:hi], op0=ALU.mult, op1=ALU.mult).then_inc(shift_made, 1)
                if t.within(NT):
                    unit_max(1)
                    unit_sub(1)
                if rear.within(NT):
                    k = rear.r
                    dve.wait_ge(logits_made, rear.n + 1)
                    if due(rear.n):
                        dve.wait_ge(ex_made, rear.n)
                    dve.tensor_copy(logits[:, :], logits_p).then_inc(logits_copied, 1)
                    dve.wait_ge(logits_copied, rear.n + 1)
                    settle(dve, turns)
                    dve.max(top[:, :], logits[:, :]).then_inc(top_made, 1)
                    dve.wait_ge(top_made, rear.n + 1)
                    dve.tensor_scalar(neg_top[:, :], top[:, 0:1], -1.0, None, ALU.mult).then_inc(neg_made, 1)
                    if due(rear.n):
                        dve.wait_ge(mask_made, rear.n)
                    settle(dve, turns)
                    dve.match_replace(without[:, :], top[:, :], logits[:, :], -3.0e38).then_inc(without_made, 1)
                    dve.wait_ge(without_made, rear.n + 1)
                    if due(rear.n):
                        dve.wait_ge(counted, rear.n)
                    dve.tensor_tensor(mask[:, :], without[:, :], logits[:, :], ALU.not_equal).then_inc(mask_made, 1)
                if front.within(NT):
                    dve.wait_ge(q_hi, front.n + 1)
                    for jj in range(2):
                        last = dve.tensor_tensor(q_parts[:, :, jj, 1:4:2, :].bitcast(F32R), query_source(jj),
                                                 q_parts[:, :, jj, 0:4:2, :], ALU.subtract)
                    last.then_inc(q_lo, 1)
                if rear.within(NT):
                    if due(16 * K * rear.q):
                        dve.wait_ge(sent[k], 16 * K * rear.q)
                    dve.tensor_scalar(row[k][:, ROW - 1:ROW].bitcast(I32), row[k][:, ROW - 1:ROW].bitcast(I32),
                                      float(2 * P), None, ALU.add).then_inc(row_named, 1)
                    dve.wait_ge(mask_made, rear.n + 1)
                    dve.wait_ge(ex_made, rear.n + 1)
                    if due(rear.n):
                        dve.wait_ge(row_weighted, rear.n)
                    dve.tensor_tensor_reduce(chosen[:, :], ex[:, :], mask[:, :], 1.0, 0.0, ALU.mult, ALU.add,
                                             w_sum[:, :]).then_inc(chosen_made, 1)
                    dve.wait_ge(chosen_made, rear.n + 1)
                    dve.reciprocal(w_inv[:, :], w_sum[:, :]).then_inc(w_inv_made, 1)
                    dve.wait_ge(w_inv_made, rear.n + 1)
                    dve.tensor_scalar(row[k][:, E:E + NX], chosen[:, :], w_inv[:, 0:1], None,
                                      ALU.mult).then_inc(row_weighted, 1)
                    dve.wait_ge(counted, rear.n + 1)
                    if due(rear.n):
                        dve.wait_ge(key_made, rear.n)
                    if due(rear.n):
                        dve.wait_ge(base_moved, rear.n)
                    dve.tensor_tensor(key_free[:, :], key_base[:, :], before_p, ALU.subtract).then_inc(free_made, 1)
                    dve.wait_ge(free_made, rear.n + 1)
                    dve.tensor_tensor(key_base[:, :], key_base[:, :], tile_p, ALU.subtract).then_inc(base_moved, 1)
                    if due(rear.n):
                        dve.wait_ge(key8_made, rear.n)
                    dve.tensor_tensor(key[:, :], key_free[:, :], mask[:, :], ALU.mult).then_inc(key_made, 1)
                    dve.wait_ge(key_made, rear.n + 1)
                    if due(rear.n):
                        dve.wait_ge(slots_made, rear.n)
                    settle(dve, turns)
                    dve.max(key8[:, :], key[:, :]).then_inc(key8_made, 1)
                    dve.wait_ge(key8_made, rear.n + 1)
                    dve.tensor_scalar(slot[k][:, :], key8[:, :], -1.0, float(KEY0), ALU.mult,
                                      ALU.add).then_inc(slots_made, 1)
            run_frames(dve, frame, 2, -2, 2, 30, NT)

            steps = [0]

            def then(ins):
                steps[0] += 1
                ins.then_inc(table_step, 1)
                dve.wait_ge(table_step, steps[0])
            dve.wait_ge(base_moved, NT)
            then(dve.tensor_tensor(count[:, :], cc("key0"), key_base[:, :], ALU.subtract))
            then(dve.tensor_scalar(count[:, :], count[:, :], float(CAP), None, ALU.min))
            wide = [P, NX, CAP // P]
            then(dve.tensor_tensor(count_le[:, :, :], count[:, :].unsqueeze(2).broadcast_to(wide),
                                   cc("steps").unsqueeze(1).broadcast_to(wide), ALU.is_gt))
            then(dve.tensor_reduce(tiles[:, :], count_le[:, :, :], AX.X, ALU.add))
            then(dve.tensor_tensor_scan(tiles_end[:, :], cc("ones")[:, 0:NX], tiles[:, :], 0.0, ALU.mult, ALU.add))
            wide = [P, NCH, NX]
            then(dve.tensor_tensor(past[:, :, :], tiles_end[:, :].unsqueeze(1).broadcast_to(wide),
                                   cc("tile").unsqueeze(2).broadcast_to(wide), ALU.is_le))
            then(dve.tensor_reduce(expert[:, :], past[:, :, :], AX.X, ALU.add))
            then(dve.tensor_tensor(past_tiles[:, :, :], past[:, :, :], tiles[:, :].unsqueeze(1).broadcast_to(wide),
                                   ALU.mult))
            then(dve.tensor_reduce(begun[:, :], past_tiles[:, :, :], AX.X, ALU.add))
            then(dve.tensor_scalar(live[:, :], expert[:, :], float(NX), float(P), ALU.is_lt, ALU.mult))
            then(dve.tensor_tensor(inside[:, :], cc("tile"), begun[:, :], ALU.subtract))
            then(dve.tensor_tensor(inside[:, :], inside[:, :], live[:, :], ALU.mult))
            then(dve.scalar_tensor_tensor(out=values[:, 0, :], in0=expert[:, :], scalar=float(REGION),
                                          in1=inside[:, :], op0=ALU.mult, op1=ALU.add))
            then(dve.tensor_scalar(values[:, 1, :], expert[:, :], float(NX - 1), None, ALU.min))
            dve.tensor_tensor(pad_f[:, :], count[:, :], cc("ebase"), ALU.add).then_inc(values_made, 1)
            dve.wait_ge(values_made, 1)
            dve.tensor_copy(pad_at[:, :], pad_f[0:1, :]).then_inc(tiles_known, 1)
            dve.wait_ge(values_turned, 1)
            dve.tensor_copy(tile_rows[:, :], bank(0)[0:1, 0:NCH * P]).then_inc(tiles_known, 1)
            dve.tensor_copy(tile_experts[:, 4:4 + NCH * P], bank(1)[0:1, 0:NCH * P]).then_inc(tiles_known, 1)
            dve.tensor_copy(expert_of[:, :], bank(1)[:, 0:NCH * P]).then_inc(tiles_known, 1)
            dve.wait_ge(tiles_known, 4)
            dve.tensor_copy(pad_f[0:1, 0:1], pad_f[0:1, 0:1]).then_inc(routed, 1)

            dve.wait_ge(routed, 2)
            for g in range(NGRP):
                dve.wait_ge(down_hi, g + 1)
                wide = slice(WG * E * g, WG * E * (g + 1))
                dve.tensor_tensor(w_dn[1][:, wide], w_dn[1][:, wide].bitcast(F32), w_dn[0][:, wide].bitcast(F32),
                                  ALU.subtract).then_inc(down_lo, 1)

            def frame_b(s):
                f, h = s.at(1), s.at(-1)
                if f.within(NS):
                    dve.wait_ge(rows_in[f.r], 32 * (f.q + 1))
                    if due(f.n - 1):
                        dve.wait_ge(weight_made, f.n - 1)
                    for i in range(2):
                        last = dve.scalar_tensor_tensor(
                            out=weights[f.r % 2][:, i, :], in0=cc("number"),
                            scalar=expert_of[:, bass.ds(f.n * 2 + i, 1)], in1=rows[f.r][:, i, E:E + NX],
                            op0=ALU.is_equal, op1=ALU.mult)
                    last.then_inc(weights_made, 1)
                    dve.tensor_copy(tokens[:, bass.ds(f.n * 2, 2)],
                                    rows[f.r][:, :, ROW - 1].bitcast(U32)).then_inc(tokens_made, 1)
                    dve.wait_ge(weights_made, f.n + 1)
                    if due(f.n - 1):
                        dve.wait_ge(inner_made, f.n - 1)
                    dve.tensor_reduce(weight[f.r % 2][:, :], weights[f.r % 2][:, :, :], AX.X,
                                      ALU.add).then_inc(weight_made, 1)
                    dve.wait_ge(x_hi, f.n + 1)
                    dve.tensor_tensor(x_t[1][f.r % 2][:, :, :, :].rearrange("p i c t -> p (i c t)"), x_t_p[f.r % 2],
                                      x_t[0][f.r % 2][:, :, :, :].rearrange("p i c t -> p (i c t)").bitcast(F32),
                                      ALU.subtract).then_inc(x_lo, 1)
                if s.within(NS):
                    dve.wait_ge(gated_made, s.n + 1)
                    dve.wait_ge(weight_made, s.n + 1)
                    if due(s.n - 1):
                        dve.wait_ge(h_turned, s.n - 1)
                    for i in range(2):
                        last = dve.scalar_tensor_tensor(
                            out=inner[s.r % 2][:, i, :], in0=gated[s.r % 2][:, i, :],
                            scalar=weight[s.r % 2][:, i:i + 1],
                            in1=gu_p[s.r % 2][:, 2 * I * i + I:2 * I * (i + 1)], op0=ALU.mult, op1=ALU.mult)
                    last.then_inc(inner_made, 1)
                if h.within(NS):
                    dve.wait_ge(h_hi, h.n + 1)
                    dve.tensor_tensor(h_t[1][h.r % 2][:, :, :].rearrange("i k t -> i (k t)"), h_t_p[h.r % 2][0:I, 0:2 * P],
                                      h_t[0][h.r % 2][:, :, :].rearrange("i k t -> i (k t)").bitcast(F32),
                                      ALU.subtract).then_inc(h_lo, 1)
                    for i in range(2):
                        if due(16 * (2 * h.q + h.r // 2 - 1)):
                            dve.wait_ge(added[(2 * h.r + i) % NACC], 16 * (2 * h.q + h.r // 2 - 1))
                    dve.wait_ge(tokens_made, h.n + 1)
                    settle(dve, turns)
                    dve.tensor_copy(targets[h.r][:, :],
                                    tokens[:, bass.ds(h.n * 2, 2)]).then_inc(targets_made, 1)
            run_frames(dve, frame_b, 4, -1, 4, NS - 4, NS)

            for n in range(T // P // CR):
                a = part[n % 2]
                dve.wait_ge(part_in[n % 2], 16 * NACC * (n // 2 + 1))
                dve.tensor_tensor(a[0][:, :], a[0][:, :], a[1][:, :], ALU.add).then_inc(half_sum[0], 1)
                dve.tensor_tensor(a[2][:, :], a[2][:, :], a[3][:, :], ALU.add).then_inc(half_sum[1], 1)
                if due(n + 1):
                    dve.wait_ge(half_sum[0], n + 1)
                if due(n + 1):
                    dve.wait_ge(half_sum[1], n + 1)
                dve.tensor_tensor(a[0][:, :], a[0][:, :], a[2][:, :], ALU.add).then_inc(summed, 1)

        @block.tensor
        def _(pe):
            turns = pe_turns
            pe.wait_ge(consts_in, 32)
            pe.wait_ge(consts_made, 8)

            def frame(t):
                after, front, rear = t.at(1), t.at(2), t.at(-1)

                def scores(u, n):
                    pe.wait_ge(k_masked, n.n + 1)
                    pe.wait_ge(q_copied[u], n.n + 1)
                    if due(n.n):
                        pe.wait_ge(probs_made[u], n.n)
                    for jp in (2 * u, 2 * u + 1):
                        for gp in range(2):
                            for jj in range(2):
                                for b in range(2):
                                    col = (((jp % 2) * 2 + gp) * P) + 512 * jj
                                    r = slice(64 * jj, 64 * jj + 64)
                                    last = pe.matmul(scores_p[u][:, col:col + P],
                                                     q_t[n.r][r, 2 * jp + gp, S * b:S * b + P],
                                                     k_t[n.r][r, 2 * jp + b, :, :].rearrange("r g t -> r (g t)"),
                                                     start=(b == 0), stop=(b == 1))
                    last.then_inc(scored[u], 1)

                def turn_sub(u):
                    pe.wait_ge(sub_made[u], t.n + 1)
                    flat = s_sub[u][:, :, :].rearrange("p x t -> p (x t)")
                    for n in range(8):
                        last = pe.transpose(scores_p[u][:, n * P:(n + 1) * P], flat[:, n * P:(n + 1) * P], ident)
                    last.then_inc(sub_turned[u], 1)

                def attend(u):
                    pe.wait_ge(probs_made[u], t.n + 1)
                    if u == 0:
                        pe.wait_ge(v_copied, t.n + 1)
                        if due(t.n):
                            pe.wait_ge(att_made, t.n)
                    for n in range(8):
                        jj, jp, gp = n // 4, 2 * u + (n // 2) % 2, n % 2
                        j = 4 * jj + jp
                        h = j * G + 2 * gp
                        for b in range(2):
                            last = pe.matmul(out_p[S * b:S * b + S, h:h + 2, :].rearrange("p h c -> p (h c)"),
                                             probs[u][:, n, S * b:S * b + S], v_t[t.r][:, b, j, :],
                                             start=True, stop=True)
                    last.then_inc(attended[u], 1)

                def turn_q(u):
                    if u == 0:
                        pe.wait_ge(q_lo, front.n + 1)
                        if due(front.n):
                            pe.wait_ge(q_copied[0], front.n)
                    else:
                        pe.wait_ge(k_masked, front.n + 1)
                    for n in range(4):
                        last = pe.transpose(q_turn_p[u][:, n * P:(n + 1) * P],
                                            q_parts[:, 4 * u + n, :, :, :].rearrange("t jj p f -> t (jj p f)"), ident)
                    last.then_inc(q_turned[u], 1)

                if t.within(NT):
                    scores(1, t)
                    turn_sub(0)
                    attend(0)
                if front.within(NT):
                    pe.wait_ge(k_lo, front.n + 1)
                    if due(front.n):
                        pe.wait_ge(q_copied[1], front.n)
                    for n in range(4):
                        last = pe.transpose(k_turn_p[:, n * P:(n + 1) * P],
                                            k_parts[:, n, :, :, :].rearrange("t jj p w -> t (jj p w)"), ident)
                    last.then_inc(k_turned, 1)
                if rear.within(NT):
                    pe.wait_ge(row_normed, rear.n + 1)
                    if due(rear.n):
                        pe.wait_ge(base_moved, rear.n)
                    for c in range(2):
                        last = pe.transpose(route_p[:, c * P:(c + 1) * P], row[rear.r][:, c * P:(c + 1) * P], ident)
                    last.then_inc(x2_turned, 1)
                if after.within(NT):
                    scores(0, after)
                if rear.within(NT):
                    pe.wait_ge(x2_copied, rear.n + 1)
                    for c in range(2):
                        last = pe.matmul(logits_p, x2_t[:, c, :], gw[:, c, :], start=(c == 0), stop=(c == 1))
                    last.then_inc(logits_made, 1)
                if t.within(NT):
                    turn_sub(1)
                if rear.within(NT):
                    pe.wait_ge(mask_made, rear.n + 1)
                    pe.wait_ge(logits_copied, rear.n + 1)
                    pe.matmul(before_p, tri_b[:, :], mask[:, :], start=True, stop=True)
                    pe.matmul(tile_p, ones_b[:, :], mask[:, :], start=True, stop=True).then_inc(counted, 1)
                if front.within(NT):
                    turn_q(0)
                if t.within(NT):
                    attend(1)
                if front.within(NT):
                    turn_q(1)
            run_frames(pe, frame, 2, -2, 2, 30, NT)

            pe.wait_ge(values_made, 1)
            for v in range(2):
                for c in range(NCH):
                    last = pe.matmul(bank(v)[:, c * P:(c + 1) * P], values[:, v, c:c + 1].broadcast_to([P, P]), ident,
                                     start=True, stop=True)
            last.then_inc(values_turned, 1)
            pe.wait_ge(values_turned, 1)
            pe.matmul(bank(2)[0:1, 0:1], values[:, 0, 0:1], ident[:, 0:1], start=True, stop=True).then_inc(routed, 1)
            pe.wait_ge(tiles_known, 4)
            expert_at = []

            def frame_b(s):
                f, h, b = s.at(1), s.at(-1), s.at(-2)
                if s.r == 0:
                    expert_at[:] = load_values(nc, mybir.EngineType.PE,
                                               tile_experts[0:1, bass.ds(s.q * 8, 12)], NX - 1)
                if f.within(NS):
                    pe.wait_ge(rows_in[f.r], 32 * (f.q + 1))
                    if due(f.n - 1):
                        pe.wait_ge(x_lo, f.n - 1)
                    for i in range(2):
                        for c in range(2):
                            last = pe.transpose(x_t_p[f.r % 2][:, (2 * i + c) * P:(2 * i + c + 1) * P],
                                                rows[f.r][:, i, c * P:(c + 1) * P], ident)
                    last.then_inc(x_turned, 1)
                if s.within(NS):
                    pe.wait_ge(x_lo, s.n + 1)
                    if due(s.n - 1):
                        pe.wait_ge(inner_made, s.n - 1)
                    settle(pe, turns)
                    for i in range(2):
                        at = expert_at[4 + 2 * s.r + i]
                        todo = [(c, xp, wp) for c in range(2) for xp, wp in ((0, 0), (0, 1), (1, 0))]
                        for n, (c, xp, wp) in enumerate(todo):
                            last = pe.matmul(gu_p[s.r % 2][:, 2 * I * i:2 * I * (i + 1)],
                                             x_t[xp][s.r % 2][:, i, c, :],
                                             w_gu[wp][:, c, bass.ds(at * (2 * I), 2 * I)],
                                             start=(n == 0), stop=(n == len(todo) - 1))
                    last.then_inc(gu_made, 1)
                if b.within(NS):
                    pe.wait_ge(h_lo, b.n + 1)
                    if due(b.n - 1):
                        pe.wait_ge(y_copied, b.n - 1)
                    pe.wait_ge(down_lo, NGRP)
                    settle(pe, turns)
                    for i in range(2):
                        at = expert_at[2 * s.r + i]
                        todo = ((0, 0), (0, 1), (1, 0))
                        for n, (hp, wp) in enumerate(todo):
                            last = pe.matmul(y_p[b.r % 2][:, i * E:(i + 1) * E], h_t[hp][b.r % 2][:, i, :],
                                             w_dn[wp][:, bass.ds(at * E, E)], start=(n == 0), stop=(n == 2))
                    last.then_inc(y_made, 1)
                if h.within(NS):
                    pe.wait_ge(inner_made, h.n + 1)
                    if due(h.n - 1):
                        pe.wait_ge(h_lo, h.n - 1)
                    for i in range(2):
                        last = pe.transpose(h_t_p[h.r % 2][0:I, i * P:(i + 1) * P], inner[h.r % 2][:, i, :], ident)
                    last.then_inc(h_turned, 1)
            run_frames(pe, frame_b, 4, -1, 4, NS - 4, NS + 1)


def kernel(x, ctx_512, L0_ffn_gate_w, L0_ffn_w_gate, L0_ffn_w_up, L0_ffn_w_down):
    import concourse.bacc as bacc
    from concourse.bass_utils import run_bass_kernel_spmd

    arrays = {"x": x, "ctx_in": ctx_512, "gate_w": L0_ffn_gate_w, "w_gate": L0_ffn_w_gate,
              "w_up": L0_ffn_w_up, "w_down": L0_ffn_w_down, "const": constants()}
    arrays = {name: np.ascontiguousarray(a) for name, a in arrays.items()}
    nc = bacc.Bacc("TRN2", target_bir_lowering=False, num_devices=1)
    ins = [nc.dram_tensor(name, a.shape, mybir.dt.from_np(a.dtype), kind="ExternalInput").ap()
           for name, a in arrays.items()]
    out = nc.dram_tensor("out", (B, S, E), F32, kind="ExternalOutput").ap()
    build(nc, *ins, out)
    r = run_bass_kernel_spmd(nc, [arrays], core_ids=[0])
    return r.results[0]["out"]
```

```python
from contextlib import ExitStack

import numpy as np

import concourse.bass as bass
from concourse import mybir

F32 = mybir.dt.float32
F32R = mybir.dt.float32r
BF16 = mybir.dt.bfloat16
I32 = mybir.dt.int32
U32 = mybir.dt.uint32
ALU = mybir.AluOpType
ACT = mybir.ActivationFunctionType
AX = mybir.AxisListType

P = 128
B, S, E = 64, 64, 256
KV, G, D = 8, 4, 8
T = B * S
NT = T // P
NX, K, I = 32, 8, 96
CAP = 2 * (T * K // NX)
REGION = T + P
NULL = NX * REGION
ROW = E + NX + 1
NB = -(-(T * K // P + NX) // 8) * 8
NS = NB // 2
KEY0 = 1 << 18
EPS = 1e-5
SCALE = float(D) ** -0.5
NACC = 4
VC = D + 1
WG = 4

CONST_COLS = {}
_at = 0
for _name, _width in (("ident", P), ("tri", P), ("gmask", 4), ("ebase", NX), ("key0", NX), ("tok", 4), ("pad", 1),
                      ("tile", NB // P + 1), ("steps", CAP // P), ("number", NX), ("ones", P)):
    CONST_COLS[_name] = slice(_at, _at + _width)
    _at += _width
NCONST = _at
NCH = NB // P + 1


def constants():
    c = np.zeros((P, NCONST), np.float32)
    p = np.arange(P)[:, None]
    c[:, CONST_COLS["ident"]] = p == np.arange(P)
    c[:, CONST_COLS["tri"]] = p < np.arange(P)
    c[:, CONST_COLS["gmask"]] = 2 * (p // 64) + (p % 16) // 8 == np.arange(4)
    c[:, CONST_COLS["ebase"]] = np.arange(NX) * REGION
    c[:, CONST_COLS["key0"]] = KEY0 - np.arange(NX) * REGION
    c[:, CONST_COLS["tok"]] = p + P * np.arange(4) - 4 * P
    c[:, CONST_COLS["pad"]] = T + p
    c[:, CONST_COLS["tile"]] = p + P * np.arange(NCH)
    c[:, CONST_COLS["steps"]] = P * np.arange(CAP // P)
    c[:, CONST_COLS["number"]] = np.arange(NX)
    c[:, CONST_COLS["ones"]] = 1.0
    return c


class Step:

    def __init__(self, q, r, ring):
        self.q, self.r, self.ring = q, r, ring

    def at(self, d):
        return Step(self.q + (self.r + d) // self.ring, (self.r + d) % self.ring, self.ring)

    @property
    def pair(self):
        return Step(self.q * 2 + self.r // 2, self.r % 2, 2)

    @property
    def n(self):
        return self.q * self.ring + self.r

    def within(self, count):
        return not isinstance(self.q, int) or 0 <= self.n < count


def run_frames(eng, frame, ring, first, loop_from, loop_to, last, unroll=4):
    assert (loop_to - loop_from) % unroll == 0 and unroll % ring == 0
    for n in range(first, loop_from):
        frame(Step(n // ring, n % ring, ring))
    with eng.Fori(0, (loop_to - loop_from) // unroll) as i:
        for k in range(unroll):
            n = loop_from + k
            frame(Step(i * (unroll // ring) + n // ring, n % ring, ring))
    for n in range(loop_to, last + 1):
        frame(Step(n // ring, n % ring, ring))


def due(value):
    return not isinstance(value, int) or value > 0


def at_most(value, most):
    return min(value, most) if isinstance(value, int) else value


def load_values(nc, engine, values, most):
    _, registers = nc.values_load_multi_w_load_instructions(
        values, engines=(engine,), min_val=0, max_val=most,
        skip_runtime_bounds_check_because="they are clamped as they are computed")
    return registers


def settle(eng, turns):
    eng.sem_inc(turns, 1)


def build(nc, x, ctx_in, gate_w, w_gate, w_up, w_down, const, out):
    xf = x.rearrange("b s e -> (b s) e")
    cf = ctx_in.rearrange("b s e -> (b s) e")
    outf = out.rearrange("b s e -> (b s) e")
    table = nc.dram_tensor("table", (NULL + P, ROW), F32, kind="Internal").ap()
    acc = [nc.dram_tensor(f"acc{i}", (T + P, E), F32, kind="Internal").ap() for i in range(NACC)]

    with ExitStack() as stack:
        def sem(name):
            return stack.enter_context(nc.semaphore(name))

        def sems(name, n):
            return [sem(f"{name}{i}") for i in range(n)]

        def allocate(where):
            def sb(name, shape, dt=F32):
                return where.enter_context(nc.sbuf_tensor(name, shape, dt))
            return sb

        sb = allocate(stack)
        con = sb("con", [P, NCONST])
        tri_b = sb("tri_b", [P, P], BF16)
        ones_b = sb("ones_b", [P, P], BF16)
        gw = sb("gw", [P, 2, NX])
        ident_r = sb("ident_r", [P, P], F32R)
        pad_row = sb("pad_row", [P, ROW])
        key_base = sb("key_base", [P, NX])
        w_gu = [sb(f"w_gu_{x}", [P, 2, NX * 2 * I], F32R) for x in ("hi", "lo")]
        tile_rows = sb("tile_rows", [1, NCH * P], I32)
        tile_experts = sb("tile_experts", [1, 4 + NCH * P], I32)
        expert_of = sb("expert_of", [P, NCH * P])
        pad_at = sb("pad_at", [1, NX], I32)

        def cc(name):
            return con[:, CONST_COLS[name]]
        ident = cc("ident")

        phase_a = ExitStack()
        sb = allocate(phase_a)
        stage = [sb(f"stage{i}", [P, 2, 2 * I]) for i in range(2)]
        x_q = [sb(f"x_q{i}", [P, E]) for i in range(2)]
        x_r = [sb(f"x_r{i}", [P, E]) for i in range(2)]
        ctx_t = [sb(f"ctx_t{i}", [P, KV * D]) for i in range(2)]
        ctx_v = [sb(f"ctx_v{i}", [P, 2, KV * D]) for i in range(2)]
        q_n = sb("q_n", [P, E])
        q_parts = sb("q_parts", [P, 8, 2, 4, 16], F32R)
        k_parts = sb("k_parts", [P, 4, 2, 2, 4 * D], F32R)
        q_t = [sb(f"q_t{i}", [P, 8, 3 * S], F32R) for i in range(2)]
        k_t = [sb(f"k_t{i}", [P, 8, 4, S], F32R) for i in range(2)]
        v_t = [sb(f"v_t{i}", [P, 2, KV, 2 * VC]) for i in range(2)]
        s_max = [sb(f"s_max{i}", [P, 16]) for i in range(2)]
        s_sub = [sb(f"s_sub{i}", [P, 16, S]) for i in range(2)]
        probs = [sb(f"probs{i}", [P, 8, P]) for i in range(2)]
        inv = sb("inv", [P, KV * G])
        att = sb("att", [P, E])
        stats = sb("stats", [P, 2, 6])
        mean_var = sb("mean_var", [P, 2, 2])
        var_eps = sb("var_eps", [P, 2])
        half = sb("half", [P, 2])
        rstd = sb("rstd", [P, 2])
        shift = sb("shift", [P, 2])
        x2_t = sb("x2_t", [P, 2, P])
        top = sb("top", [P, 8])
        neg_top = sb("neg_top", [P, 1])
        logits = sb("logits", [P, NX])
        ex = sb("ex", [P, NX])
        without = sb("without", [P, NX])
        mask = sb("mask", [P, NX], BF16)
        chosen = sb("chosen", [P, NX])
        w_sum = sb("w_sum", [P, 1])
        w_inv = sb("w_inv", [P, 1])
        key_free = sb("key_free", [P, NX])
        key = sb("key", [P, NX])
        key8 = sb("key8", [P, 8])
        count = sb("count", [P, NX])
        count_le = sb("count_le", [P, NX, CAP // P])
        tiles = sb("tiles", [P, NX])
        tiles_end = sb("tiles_end", [P, NX])
        past = sb("past", [P, NCH, NX])
        past_tiles = sb("past_tiles", [P, NCH, NX])
        expert = sb("expert", [P, NCH])
        begun = sb("begun", [P, NCH])
        live = sb("live", [P, NCH])
        inside = sb("inside", [P, NCH])
        values = sb("values", [P, 2, NCH])
        pad_f = sb("pad_f", [P, NX])
        x1 = [sb(f"x1_{i}", [P, E]) for i in range(2)]
        row = [sb(f"row{i}", [P, ROW]) for i in range(4)]
        zeros = sb("zeros", [P, E])
        slot = [sb(f"slot{i}", [P, 8], U32) for i in range(4)]
        phase_a.close()

        phase_b = ExitStack()
        sb = allocate(phase_b)
        w_dn = [sb(f"w_dn_{x}", [I, NX * E], F32R) for x in ("hi", "lo")]
        rows = [sb(f"rows{i}", [P, 2, ROW]) for i in range(4)]
        x_t = [[sb(f"x_t_{x}{i}", [P, 2, 2, P], F32R) for i in range(2)] for x in ("hi", "lo")]
        gated = [sb(f"gated{i}", [P, 2, I]) for i in range(2)]
        inner = [sb(f"inner{i}", [P, 2, I]) for i in range(2)]
        h_t = [[sb(f"h_t_{x}{i}", [I, 2, P], F32R) for i in range(2)] for x in ("hi", "lo")]
        y = [sb(f"y{i}", [P, 2, E]) for i in range(4)]
        weight = [sb(f"weight{i}", [P, 2]) for i in range(2)]
        weights = [sb(f"weights{i}", [P, 2, NX]) for i in range(2)]
        tokens = sb("tokens", [P, 2 * NS], U32)
        targets = [sb(f"targets{i}", [P, 2], U32) for i in range(4)]
        phase_b.close()
        phase_c = ExitStack()
        sb = allocate(phase_c)
        CR = 4
        NPART = 4
        part = [[sb(f"part{i}_{a}", [P, CR * E]) for a in range(NACC)] for i in range(NPART)]
        phase_c.close()

        psum = stack.enter_context(nc.psum_tensor("psum", [P, 8, 512], F32))

        def bank(n, k=1):
            return psum[:, n:n + k, :].rearrange("p k c -> p (k c)")
        scores_p = [bank(0, 2), bank(2, 2)]
        k_turn_p = bank(4)
        q_turn_p = [bank(5), bank(4)]
        route_p = bank(6)
        out_p = bank(7)[:, 0:KV * G * VC].rearrange("p (h c) -> p h c", c=VC)
        logits_p = route_p[:, 0:NX]
        before_p = route_p[:, 0:NX]
        tile_p = route_p[:, NX:2 * NX]
        x_t_p = [bank(0), bank(1)]
        gu_p = [bank(2), bank(3)]
        h_t_p = [bank(4), bank(7)]
        y_p = [bank(5), bank(6)]

        def key_view(jj, low):
            return k_parts[:, :, jj, low, :].rearrange("t jp (x d) -> t jp x d", d=D)

        def key_source(k, jj):
            return (ctx_t[k][:, 32 * jj:32 * jj + 32].rearrange("t (jp d) -> t jp d", d=D).unsqueeze(2)
                    .broadcast_to([P, 4, 4, D]))

        def query_source(jj):
            return (q_n[:, P * jj:P * jj + P].rearrange("t (n f) -> t n f", f=16).unsqueeze(2)
                    .broadcast_to([P, 8, 2, 16]))


        pool_turns = sem("pool_turns")
        dve_turns = sem("dve_turns")
        pe_turns = sem("pe_turns")
        act_turns = sem("act_turns")
        consts_in = sem("consts_in")
        consts_made = sem("consts_made")
        ones_made = sem("ones_made")
        pool_ready = sem("pool_ready")
        stage_in = sems("stage_in", 2)
        gu_hi = sem("gu_hi")
        gu_lo = sem("gu_lo")
        down_in = sems("down_in", NX // WG)
        down_hi = sem("down_hi")
        down_lo = sem("down_lo")
        x_q_in = sems("x_q_in", 2)
        x_r_in = sems("x_r_in", 2)
        ctx_in_s = sems("ctx_in_s", 2)
        ctx_v_in = sems("ctx_v_in", 2)
        x1_out = sems("x1_out", 2)
        zero_out = sem("zero_out")
        null_out = sem("null_out")
        k_hi = sem("k_hi")
        k_lo = sem("k_lo")
        k_turned = sem("k_turned")
        k_masked = sem("k_masked")
        v_copied = sem("v_copied")
        scored = sems("scored", 2)
        max_made = sems("max_made", 2)
        sub_made = sems("sub_made", 2)
        sub_turned = sems("sub_turned", 2)
        probs_made = sems("probs_made", 2)
        attended = sems("attended", 2)
        stats1 = sem("stats1")
        stats2 = sem("stats2")
        aggr1 = sem("aggr1")
        aggr2 = sem("aggr2")
        var_made = sem("var_made")
        rstd_made = sem("rstd_made")
        shift_made = sem("shift_made")
        inv_made = sem("inv_made")
        att_made = sem("att_made")
        x1_made = sem("x1_made")
        q_normed = sem("q_normed")
        q_hi = sem("q_hi")
        q_lo = sem("q_lo")
        q_turned = sems("q_turned", 2)
        q_copied = sems("q_copied", 2)
        row_normed = sem("row_normed")
        row_weighted = sem("row_weighted")
        row_named = sem("row_named")
        x2_turned = sem("x2_turned")
        x2_copied = sem("x2_copied")
        logits_made = sem("logits_made")
        logits_copied = sem("logits_copied")
        top_made = sem("top_made")
        neg_made = sem("neg_made")
        ex_made = sem("ex_made")
        without_made = sem("without_made")
        mask_made = sem("mask_made")
        chosen_made = sem("chosen_made")
        w_inv_made = sem("w_inv_made")
        counted = sem("counted")
        free_made = sem("free_made")
        key_made = sem("key_made")
        base_moved = sem("base_moved")
        key8_made = sem("key8_made")
        slots_made = sem("slots_made")
        sent = sems("sent", 4)
        routed = sem("routed")
        table_step = sem("table_step")
        values_made = sem("values_made")
        values_turned = sem("values_turned")
        tiles_known = sem("tiles_known")
        pads_out = sem("pads_out")

        rows_in = sems("rows_in", 4)
        x_turned = sem("x_turned")
        x_hi = sem("x_hi")
        x_lo = sem("x_lo")
        weight_made = sem("weight_made")
        weights_made = sem("weights_made")
        tokens_made = sem("tokens_made")
        targets_made = sem("targets_made")
        gu_made = sem("gu_made")
        gated_made = sem("gated_made")
        inner_made = sem("inner_made")
        h_turned = sem("h_turned")
        h_hi = sem("h_hi")
        h_lo = sem("h_lo")
        y_made = sem("y_made")
        y_copied = sem("y_copied")
        added = sems("added", NACC)
        part_in = sems("part_in", NPART)
        half_sum = sems("half_sum", 2)
        summed = sem("summed")
        out_done = sems("out_done", NPART)

        NGRP = NX // WG
        ZEROS = (NACC - 1) * NT + NACC
        assert NX == NT and KV * D == 64
        block = stack.enter_context(nc.Block())

        @block.sync
        def _(sp):
            sp.dma_start(con[:, :], const).then_inc(consts_in, 16)
            sp.dma_start(gw[:, :, :], gate_w.rearrange("(c p) e -> p c e", p=P)).then_inc(consts_in, 16)

            def load_weights(e):
                if due(e.n - 1):
                    sp.wait_ge(gu_lo, e.n - 1)
                for m, w in enumerate((w_gate, w_up)):
                    sp.dma_start(stage[e.r][:, :, I * m:I * (m + 1)],
                                 w[bass.ds(e.n, 1), :, :].rearrange("o (c p) i -> p (o c) i", p=P)
                                 ).then_inc(stage_in[e.r], 16)

            def load_front(t):
                k = t.r
                if due(t.n - 1):
                    sp.wait_ge(q_normed, t.n - 1)
                sp.dma_start(x_q[k][:, :], xf[bass.ds(t.n * P, P), :]).then_inc(x_q_in[k], 16)
                if due(t.n - 1):
                    sp.wait_ge(k_lo, 2 * (t.n - 1))
                sp.dma_start(ctx_t[k][:, :], cf[bass.ds(t.n * P, P), :]).then_inc(ctx_in_s[k], 16)

            def load_values_of(t):
                k = t.r
                if due(t.n - 1):
                    sp.wait_ge(v_copied, t.n - 1)
                for g in range(2):
                    sp.dma_start(ctx_v[k][S * g:S * g + S, :, :],
                                 cf[bass.ds(t.n * P, P), :].rearrange("(b t) f -> t b f", b=2)
                                 ).then_inc(ctx_v_in[k], 16)

            def frame(t):
                if t.at(3).within(NT):
                    load_front(t.at(3))
                if t.at(2).within(NT):
                    load_values_of(t.at(2))
                if t.at(1).within(NX):
                    load_weights(t.at(1))
                if t.within(NT):
                    if due(t.n - 1):
                        sp.wait_ge(x1_made, t.n - 1)
                    sp.dma_start(x_r[t.r][:, :], xf[bass.ds(t.n * P, P), :]).then_inc(x_r_in[t.r], 16)
                    for a in range(1, NACC):
                        sp.dma_start(acc[a][bass.ds(t.n * P, P), :], zeros[:, :]).then_inc(zero_out, 16)
                if t.at(-1).within(NT):
                    u = t.at(-1)
                    sp.wait_ge(x1_made, u.n + 1)
                    sp.dma_start(acc[0][bass.ds(u.n * P, P), :], x1[u.r][:, :]).then_inc(x1_out[u.r], 16)

            frame(Step(-2, 1, 2))
            frame(Step(-1, 0, 2))
            frame(Step(-1, 1, 2))
            sp.wait_ge(pool_ready, 3)
            for a in range(NACC):
                sp.dma_start(acc[a][T:T + P, :], zeros[:, :]).then_inc(zero_out, 16)
            sp.dma_start(table[NULL:NULL + P, :], pad_row[:, :]).then_inc(null_out, 16)
            run_frames(sp, frame, 2, 0, 1, 29, NT)

            sp.wait_ge(tiles_known, 4)
            for k in range(4):
                sp.wait_ge(sent[k], 16 * K * (NT // 4))
            for k in range(2):
                sp.wait_ge(x1_out[k], 16 * (NT // 2))
            sp.wait_ge(tiles_known, 4)
            with sp.Fori(0, NX // 16) as e:
                ats = load_values(nc, mybir.EngineType.SP, pad_at[0:1, bass.ds(e * 8, 8)], NULL - P)
                for at in ats:
                    sp.dma_start(table[bass.ds(at, P), :], pad_row[:, :]).then_inc(pads_out, 16)
            sp.wait_ge(pads_out, 16 * NX)
            sp.wait_ge(null_out, 16)
            sp.wait_ge(routed, 2)

            at = []

            def load_rows(s):
                if s.r == 0:
                    at[:] = load_values(nc, mybir.EngineType.SP, tile_rows[0:1, bass.ds(s.n * 2, 8)], NULL)
                if due(s.n - 3):
                    sp.wait_ge(x_turned, s.n - 3)
                if due(s.n - 3):
                    sp.wait_ge(tokens_made, s.n - 3)
                for i in range(2):
                    sp.dma_start(rows[s.r][:, i, :], table[bass.ds(at[2 * s.r + i], P), :]).then_inc(rows_in[s.r], 16)

            run_frames(sp, load_rows, 4, 0, 8, NS, NS - 1, unroll=8)

            for a in range(NACC):
                sp.wait_ge(added[a], 16 * NB // NACC)
            sp.wait_ge(zero_out, 16 * ZEROS)
            chunks = [[a_[0:T, :].rearrange("(p r) e -> p (r e)", p=P)[:, n * CR * E:(n + 1) * CR * E] for a_ in acc]
                      for n in range(T // P // CR)]
            for n in range(len(chunks)):
                if due(16 * (n // NPART)):
                    sp.wait_ge(out_done[n % NPART], 16 * (n // NPART))
                for a in range(NACC):
                    sp.dma_start(part[n % NPART][a][:, :], chunks[n][a]).then_inc(part_in[n % NPART], 16)
            for k in range(NPART):
                sp.wait_ge(out_done[k], 16 * len(chunks) // NPART)

        @block.gpsimd
        def _(pool):
            turns = pool_turns
            pool.memset(zeros[:, :], 0.0).then_inc(pool_ready, 1)
            pool.memset(half[:, :], -0.5).then_inc(pool_ready, 1)
            pool.wait_ge(consts_made, 11)
            pool.memset(pad_row[:, 0:ROW - 1], 0.0).then_inc(pool_ready, 1)
            pool.wait_ge(pool_ready, 3)

            def frame(s):
                t = s.pair

                def send(u, first, last):
                    for k in range(first, last):
                        pool.indirect_dma_start(out=table[:, :],
                                                out_offset=bass.IndirectOffsetOnAxis(ap=slot[u.r][:, k:k + 1], axis=0),
                                                in_=row[u.r][:, :], in_offset=None).then_inc(sent[u.r], 16)
                sent_first = K if isinstance(t.q, int) and t.n >= NT else K // 2
                if s.at(-4).within(NT):
                    u = s.at(-4)
                    pool.wait_ge(slots_made, u.n + 1)
                    pool.wait_ge(row_weighted, u.n + 1)
                    pool.wait_ge(row_named, u.n + 1)
                    pool.wait_ge(row_normed, u.n + 1)
                    settle(pool, turns)
                    send(u, 0, sent_first)
                lo = 0 if t.at(-1).within(NT) else 1
                hi = 2 if t.at(2).within(NT) else 1
                if lo < hi:
                    pool.wait_ge(var_made, t.n + 3)
                    if due(t.n + 2):
                        pool.wait_ge(shift_made, t.n + 2)
                    if due(t.n - 1):
                        pool.wait_ge(row_normed, t.n - 1)
                    if due(at_most(t.n + 2, NT)):
                        pool.wait_ge(q_normed, at_most(t.n + 2, NT))
                    pool.tensor_tensor(rstd[:, lo:hi], var_eps[:, lo:hi], half[:, lo:hi],
                                       ALU.pow).then_inc(rstd_made, 1)
                if s.at(-4).within(NT):
                    send(s.at(-4), sent_first, K)
            run_frames(pool, frame, 4, -2, 4, 28, NT + 3)

            pool.wait_ge(zero_out, 16 * ZEROS)
            for k in range(2):
                pool.wait_ge(x1_out[k], 16 * (NT // 2))

            def add(s):
                for i in range(2):
                    a = (2 * s.r + i) % NACC
                    if due(16 * (s.q * 2 + s.r // 2)):
                        pool.wait_ge(added[a], 16 * (s.q * 2 + s.r // 2))
                    pool.wait_ge(y_copied, s.n + 1)
                    pool.wait_ge(targets_made, s.n + 1)
                    settle(pool, turns)
                    pool.indirect_dma_start(out=acc[a][:, :],
                                            out_offset=bass.IndirectOffsetOnAxis(ap=targets[s.r][:, i:i + 1], axis=0),
                                            in_=y[s.r][:, i, :], in_offset=None,
                                            compute_op=ALU.add).then_inc(added[a], 16)
            run_frames(pool, add, 4, 0, 8, NS, NS - 1, unroll=8)

        @block.scalar
        def _(act):
            turns = act_turns
            act.wait_ge(consts_in, 32)
            act.wait_ge(ones_made, 6)

            def frame(s):
                t = s.pair
                front, rear, chosen_t, placed_t = t.at(2), t.at(-1), t.at(-2), t.at(-3)
                def probabilities(u):
                    act.wait_ge(sub_turned[u], t.n + 1)
                    if due(t.n):
                        act.wait_ge(attended[u], t.n)
                    act.activation(probs[u][:, :, :].rearrange("p x s -> p (x s)"), scores_p[u],
                                   ACT.Exp, scale=SCALE).then_inc(probs_made[u], 1)
                if placed_t.within(NT):
                    act.wait_ge(neg_made, placed_t.n + 1)
                    if due(placed_t.n):
                        act.wait_ge(chosen_made, placed_t.n)
                    act.activation(ex[:, :], logits[:, :], ACT.Exp, bias=neg_top[:, 0:1]).then_inc(ex_made, 1)
                if t.within(NX):
                    act.wait_ge(stage_in[t.r], 32 * (t.q + 1))
                    settle(act, turns)
                    act.copy(w_gu[0][:, :, bass.ds(t.n * (2 * I), 2 * I)], stage[t.r][:, :, :]).then_inc(gu_hi, 1)
                if front.within(NT):
                    k = front.r
                    act.wait_ge(ctx_in_s[k], 16 * (front.q + 1))
                    if due(front.n):
                        act.wait_ge(k_turned, front.n)
                    for jj in range(2):
                        last = act.copy(key_view(jj, 0), key_source(k, jj))
                    last.then_inc(k_hi, 1)
                if t.at(1).within(NT):
                    n = t.at(1)
                    act.wait_ge(ctx_v_in[n.r], 32 * (n.q + 1))
                    for u in range(2):
                        if due(n.n - 1):
                            act.wait_ge(attended[u], n.n - 1)
                    for g in range(2):
                        half_p = slice(S * g, S * g + S)
                        last = act.copy(v_t[n.r][half_p, :, :, VC * g:VC * g + D].rearrange("t b j d -> t (b j) d"),
                                        ctx_v[n.r][half_p, :, :].rearrange("t b (j d) -> t (b j) d", d=D))
                    last.then_inc(v_copied, 1)

                if t.within(NT):
                    probabilities(0)
                if rear.within(NT):
                    k = s.at(-1)
                    act.wait_ge(shift_made, t.n + 3)
                    if due(16 * K * k.q):
                        act.wait_ge(sent[k.r], 16 * K * k.q)
                    act.activation(row[k.r][:, 0:E], x1[rear.r][:, :], ACT.Identity, bias=shift[:, 0:1],
                                   scale=rstd[:, 0:1]).then_inc(row_normed, 1)
                if front.within(NT):
                    k = front.r
                    act.wait_ge(shift_made, t.n + 3)
                    if due(front.n):
                        act.wait_ge(q_lo, 2 * front.n)
                    act.activation(q_n[:, :], x_q[k][:, :], ACT.Identity, bias=shift[:, 1:2],
                                   scale=rstd[:, 1:2]).then_inc(q_normed, 1)
                    act.wait_ge(q_normed, front.n + 1)
                    for u in range(2):
                        if due(front.n):
                            act.wait_ge(q_turned[u], front.n)
                    for jj in range(2):
                        last = act.copy(q_parts[:, :, jj, 0:4:2, :], query_source(jj))
                    last.then_inc(q_hi, 1)
                if chosen_t.within(NT):
                    act.wait_ge(x2_turned, chosen_t.n + 1)
                    if due(chosen_t.n):
                        act.wait_ge(logits_made, chosen_t.n)
                    act.copy(x2_t[:, :, :].rearrange("p c t -> p (c t)"), route_p[:, 0:E]).then_inc(x2_copied, 1)
                if front.within(NT):
                    k = front.r
                    act.wait_ge(k_turned, front.n + 1)
                    for u in range(2):
                        if due(front.n - 1):
                            act.wait_ge(scored[u], front.n - 1)
                    for g in range(4):
                        last = act.activation(k_t[k][:, :, g, :], k_turn_p.rearrange("r (x t) -> r x t", t=S),
                                              ACT.Copy, scale=cc("gmask")[:, g:g + 1])
                    last.then_inc(k_masked, 1)
                if t.within(NT):
                    probabilities(1)
                if front.within(NT):
                    for u in range(2):
                        act.wait_ge(q_turned[u], front.n + 1)
                        if due(front.n - 1):
                            act.wait_ge(scored[u], front.n - 1)
                        src = q_turn_p[u].rearrange("r (c b s) -> r c b s", b=2, s=S)
                        dst = q_t[front.r][:, 4 * u:4 * u + 4, :].rearrange("r c (b s) -> r c b s", b=3)[:, :, 0:3:2, :]
                        act.copy(dst, src).then_inc(q_copied[u], 1)

            run_frames(act, frame, 4, -2, 3, 27, NT + 2)

            act.wait_ge(routed, 2)
            for g in range(NGRP):
                wide = slice(WG * E * g, WG * E * (g + 1))
                act.dma_start(w_dn[1][:, wide].bitcast(F32).rearrange("i (e h) -> i e h", h=E),
                              w_down[WG * g:WG * g + WG, :, :].rearrange("e i h -> i e h")).then_inc(down_in[g], 16)
            for g in range(NGRP):
                wide = slice(WG * E * g, WG * E * (g + 1))
                act.wait_ge(down_in[g], 16)
                act.copy(w_dn[0][:, wide], w_dn[1][:, wide].bitcast(F32)).then_inc(down_hi, 1)

            for k in range(4):
                act.wait_ge(sent[k], 16 * K * (NT // 4))
            act.wait_ge(tiles_known, 4)
            with act.Fori(NX // 16, NX // 8) as e:
                ats = load_values(nc, mybir.EngineType.Activation, pad_at[0:1, bass.ds(e * 8, 8)], NULL - P)
                for at in ats:
                    act.dma_start(table[bass.ds(at, P), :], pad_row[:, :]).then_inc(pads_out, 16)

            def frame_b(s):
                f, h, b = s.at(1), s.at(-1), s.at(-2)
                if f.within(NS):
                    act.wait_ge(x_turned, f.n + 1)
                    if due(f.n - 1):
                        act.wait_ge(gu_made, f.n - 1)
                    act.copy(x_t[0][f.r % 2][:, :, :, :].rearrange("p i c t -> p (i c t)"),
                             x_t_p[f.r % 2]).then_inc(x_hi, 1)
                if s.within(NS):
                    act.wait_ge(gu_made, s.n + 1)
                    if due(s.n - 1):
                        act.wait_ge(inner_made, s.n - 1)
                    act.activation(gated[s.r % 2][:, :, :],
                                   gu_p[s.r % 2][:, 0:4 * I].rearrange("p (i w) -> p i w", i=2)[:, :, 0:I],
                                   ACT.Silu).then_inc(gated_made, 1)
                if b.within(NS):
                    act.wait_ge(y_made, b.n + 1)
                    for i in range(2):
                        if due(16 * (b.q * 2 + b.r // 2 - 1)):
                            act.wait_ge(added[(2 * b.r + i) % NACC], 16 * (b.q * 2 + b.r // 2 - 1))
                    act.copy(y[b.r][:, :, :].rearrange("p i e -> p (i e)"), y_p[b.r % 2]).then_inc(y_copied, 1)
                if h.within(NS):
                    act.wait_ge(h_turned, h.n + 1)
                    if due(h.n - 1):
                        act.wait_ge(y_made, h.n - 1)
                    act.copy(h_t[0][h.r % 2][:, :, :].rearrange("i k t -> i (k t)"),
                             h_t_p[h.r % 2][0:I, 0:2 * P]).then_inc(h_hi, 1)
            run_frames(act, frame_b, 4, -1, 4, NS - 12, NS + 1, unroll=16)

            final = [outf.rearrange("(p r) e -> p (r e)", p=P)[:, n * CR * E:(n + 1) * CR * E]
                     for n in range(T // P // CR)]
            for n in range(len(final)):
                act.wait_ge(summed, n + 1)
                act.dma_start(final[n], part[n % NPART][0][:, :]).then_inc(out_done[n % NPART], 16)

        @block.vector
        def _(dve):
            turns = dve_turns
            dve.wait_ge(consts_in, 32)
            dve.tensor_copy(tri_b[:, :], cc("tri")).then_inc(consts_made, 1)
            dve.tensor_copy(ones_b[:, :], cc("ones")).then_inc(consts_made, 1)
            dve.tensor_copy(ident_r[:, :], ident).then_inc(consts_made, 1)
            dve.tensor_copy(key_base[:, :], cc("key0")).then_inc(consts_made, 1)
            dve.tensor_copy(pad_row[:, ROW - 1:ROW].bitcast(U32), cc("pad")).then_inc(consts_made, 1)
            for k in range(4):
                dve.tensor_copy(row[k][:, ROW - 1:ROW].bitcast(I32), cc("tok")[:, k:k + 1]).then_inc(consts_made, 1)
            dve.memset(stats[:, :, :], 0.0).then_inc(consts_made, 1)
            for k in range(2):
                if k == 0:
                    dve.memset(tile_experts[:, 0:4], 0).then_inc(consts_made, 1)
                dve.memset(q_t[k][:, :, S:2 * S].bitcast(F32), 0.0).then_inc(ones_made, 1)
                dve.memset(v_t[k][:, :, :, :], 0.0).then_inc(ones_made, 1)
            dve.wait_ge(ones_made, 4)
            for k in range(2):
                for g in range(2):
                    last = dve.memset(v_t[k][S * g:S * g + S, :, :, VC * g + D:VC * g + VC], 1.0)
                last.then_inc(ones_made, 1)
            def frame(s):
                t = s.pair
                front, rear, chosen_t, placed_t = t.at(2), t.at(-1), t.at(-2), t.at(-3)

                def unit_max(u):
                    dve.wait_ge(scored[u], t.n + 1)
                    if due(t.n):
                        dve.wait_ge(sub_made[u], t.n)
                    dve.tensor_reduce(s_max[u][:, :], scores_p[u].rearrange("p (x t) -> p x t", t=S),
                                      AX.X, ALU.max).then_inc(max_made[u], 1)

                def unit_sub(u):
                    dve.wait_ge(max_made[u], t.n + 1)
                    if due(t.n):
                        dve.wait_ge(sub_turned[u], t.n)
                    dve.tensor_tensor(s_sub[u][:, :, :], scores_p[u].rearrange("p (x t) -> p x t", t=S),
                                      s_max[u][:, :].unsqueeze(2).broadcast_to([P, 16, S]),
                                      ALU.subtract).then_inc(sub_made[u], 1)

                def keys_low(jj):
                    if jj == 0:
                        dve.wait_ge(k_hi, front.n + 1)
                    dve.tensor_tensor(key_view(jj, 1), key_source(front.r, jj), key_view(jj, 0).bitcast(F32),
                                      ALU.subtract).then_inc(k_lo, 1)

                def queries_low(jj):
                    if jj == 0:
                        dve.wait_ge(q_hi, front.n + 1)
                    dve.tensor_tensor(q_parts[:, :, jj, 1:4:2, :], query_source(jj),
                                      q_parts[:, :, jj, 0:4:2, :].bitcast(F32), ALU.subtract).then_inc(q_lo, 1)

                lo = 0 if rear.within(NT) else 1
                hi = 2 if front.within(NT) else 1
                if t.within(NT):
                    unit_max(0)
                    unit_sub(0)
                if rear.within(NT):
                    for u in range(2):
                        dve.wait_ge(attended[u], rear.n + 1)
                    if due(rear.n):
                        dve.wait_ge(att_made, rear.n)
                    dve.reciprocal(inv[:, :], out_p[:, :, D]).then_inc(inv_made, 1)
                if placed_t.within(NT):
                    dve.wait_ge(mask_made, placed_t.n + 1)
                    dve.wait_ge(ex_made, placed_t.n + 1)
                    if due(placed_t.n):
                        dve.wait_ge(row_weighted, placed_t.n)
                    dve.tensor_tensor_reduce(chosen[:, :], ex[:, :], mask[:, :], 1.0, 0.0, ALU.mult, ALU.add,
                                             w_sum[:, :]).then_inc(chosen_made, 1)
                if rear.within(NT):
                    dve.wait_ge(inv_made, rear.n + 1)
                    if due(rear.n):
                        dve.wait_ge(x1_made, rear.n)
                    dve.tensor_tensor(att[:, :].rearrange("p (h d) -> p h d", d=D), out_p[:, :, 0:D],
                                      inv[:, :].unsqueeze(2).broadcast_to([P, KV * G, D]),
                                      ALU.mult).then_inc(att_made, 1)
                if placed_t.within(NT):
                    dve.wait_ge(counted, placed_t.n + 1)
                    if due(placed_t.n):
                        dve.wait_ge(key_made, placed_t.n)
                        dve.wait_ge(base_moved, placed_t.n)
                    dve.tensor_tensor(key_free[:, :], key_base[:, :], before_p, ALU.subtract).then_inc(free_made, 1)
                    dve.wait_ge(free_made, placed_t.n + 1)
                    if due(placed_t.n):
                        dve.wait_ge(key8_made, placed_t.n)
                    dve.tensor_tensor(key[:, :], key_free[:, :], mask[:, :], ALU.mult).then_inc(key_made, 1)
                    dve.tensor_tensor(key_base[:, :], key_base[:, :], tile_p, ALU.subtract).then_inc(base_moved, 1)
                if front.within(NT):
                    k = front.r
                    dve.wait_ge(x_q_in[k], 16 * (front.q + 1))
                    if due(front.n):
                        dve.wait_ge(aggr1, front.n)
                    dve.bn_stats(stats[:, 1, :], x_q[k][:, :]).then_inc(stats1, 1)
                if rear.within(NT):
                    k = rear.r
                    dve.wait_ge(att_made, rear.n + 1)
                    dve.wait_ge(x_r_in[k], 16 * (rear.q + 1))
                    if due(16 * rear.q):
                        dve.wait_ge(x1_out[k], 16 * rear.q)
                    if due(rear.n - 1):
                        dve.wait_ge(row_normed, rear.n - 1)
                    dve.tensor_tensor(x1[k][:, :], att[:, :], x_r[k][:, :], ALU.add).then_inc(x1_made, 1)
                if front.within(NT):
                    dve.wait_ge(stats1, front.n + 1)
                    if due(t.n + 2):
                        dve.wait_ge(shift_made, t.n + 2)
                    settle(dve, turns)
                    dve.bn_aggr(mean_var[:, 1, :], stats[:, 1, :]).then_inc(aggr1, 1)
                if rear.within(NT):
                    dve.wait_ge(x1_made, rear.n + 1)
                    if due(rear.n):
                        dve.wait_ge(aggr2, rear.n)
                    dve.bn_stats(stats[:, 0, :], x1[rear.r][:, :]).then_inc(stats2, 1)
                if placed_t.within(NT):
                    dve.wait_ge(chosen_made, placed_t.n + 1)
                    dve.reciprocal(w_inv[:, :], w_sum[:, :]).then_inc(w_inv_made, 1)
                    dve.wait_ge(key_made, placed_t.n + 1)
                    if due(placed_t.n):
                        dve.wait_ge(slots_made, placed_t.n)
                    settle(dve, turns)
                    dve.max(key8[:, :], key[:, :]).then_inc(key8_made, 1)
                if rear.within(NT):
                    dve.wait_ge(stats2, rear.n + 1)
                    if due(t.n + 2):
                        dve.wait_ge(shift_made, t.n + 2)
                    settle(dve, turns)
                    dve.bn_aggr(mean_var[:, 0, :], stats[:, 0, :]).then_inc(aggr2, 1)
                if placed_t.within(NT):
                    k = s.at(-3)
                    dve.wait_ge(w_inv_made, placed_t.n + 1)
                    dve.tensor_scalar(row[k.r][:, E:E + NX], chosen[:, :], w_inv[:, 0:1], None,
                                      ALU.mult).then_inc(row_weighted, 1)
                if lo < hi:
                    if rear.within(NT):
                        dve.wait_ge(aggr2, rear.n + 1)
                    if front.within(NT):
                        dve.wait_ge(aggr1, front.n + 1)
                    if due(t.n + 2):
                        dve.wait_ge(rstd_made, t.n + 2)
                    dve.tensor_scalar(var_eps[:, lo:hi], mean_var[:, lo:hi, 1], EPS, None,
                                      ALU.add).then_inc(var_made, 1)
                if placed_t.within(NT):
                    k = s.at(-3)
                    dve.wait_ge(key8_made, placed_t.n + 1)
                    dve.tensor_scalar(slot[k.r][:, :], key8[:, :], -1.0, float(KEY0), ALU.mult,
                                      ALU.add).then_inc(slots_made, 1)
                if front.within(NT):
                    keys_low(0)
                    keys_low(1)
                if t.within(NT):
                    unit_max(1)
                if lo < hi:
                    dve.wait_ge(rstd_made, t.n + 3)
                    if due(rear.n):
                        dve.wait_ge(row_normed, rear.n)
                    if due(at_most(t.n + 2, NT)):
                        dve.wait_ge(q_normed, at_most(t.n + 2, NT))
                    dve.scalar_tensor_tensor(out=shift[:, lo:hi], in0=mean_var[:, lo:hi, 0], scalar=-1.0,
                                             in1=rstd[:, lo:hi], op0=ALU.mult, op1=ALU.mult).then_inc(shift_made, 1)
                if t.within(NT):
                    unit_sub(1)
                if t.within(NX):
                    dve.wait_ge(gu_hi, t.n + 1)
                    settle(dve, turns)
                    wide = bass.ds(t.n * (2 * I), 2 * I)
                    dve.tensor_tensor(w_gu[1][:, :, wide], stage[t.r][:, :, :], w_gu[0][:, :, wide].bitcast(F32),
                                      ALU.subtract).then_inc(gu_lo, 1)
                if chosen_t.within(NT):
                    dve.wait_ge(logits_made, chosen_t.n + 1)
                    if due(chosen_t.n):
                        dve.wait_ge(ex_made, chosen_t.n)
                    dve.tensor_copy(logits[:, :], logits_p).then_inc(logits_copied, 1)
                if placed_t.within(NT):
                    k = s.at(-3)
                    if due(16 * K * k.q):
                        dve.wait_ge(sent[k.r], 16 * K * k.q)
                    dve.tensor_scalar(row[k.r][:, ROW - 1:ROW].bitcast(I32), row[k.r][:, ROW - 1:ROW].bitcast(I32),
                                      float(4 * P), None, ALU.add).then_inc(row_named, 1)
                if front.within(NT):
                    queries_low(0)
                if chosen_t.within(NT):
                    dve.wait_ge(logits_copied, chosen_t.n + 1)
                    settle(dve, turns)
                    dve.max(top[:, :], logits[:, :]).then_inc(top_made, 1)
                    dve.wait_ge(top_made, chosen_t.n + 1)
                    dve.tensor_scalar(neg_top[:, :], top[:, 0:1], -1.0, None, ALU.mult).then_inc(neg_made, 1)
                    if due(chosen_t.n):
                        dve.wait_ge(mask_made, chosen_t.n)
                    settle(dve, turns)
                    dve.match_replace(without[:, :], top[:, :], logits[:, :], -3.0e38).then_inc(without_made, 1)
                if front.within(NT):
                    queries_low(1)
                if chosen_t.within(NT):
                    dve.wait_ge(without_made, chosen_t.n + 1)
                    if due(chosen_t.n):
                        dve.wait_ge(counted, chosen_t.n)
                    dve.tensor_tensor(mask[:, :], without[:, :], logits[:, :], ALU.not_equal).then_inc(mask_made, 1)
            run_frames(dve, frame, 4, -2, 3, 27, NT + 2)

            steps = [0]

            def then(ins):
                steps[0] += 1
                ins.then_inc(table_step, 1)
                dve.wait_ge(table_step, steps[0])
            dve.wait_ge(base_moved, NT)
            then(dve.tensor_tensor(count[:, :], cc("key0"), key_base[:, :], ALU.subtract))
            then(dve.tensor_scalar(count[:, :], count[:, :], float(CAP), None, ALU.min))
            wide = [P, NX, CAP // P]
            then(dve.tensor_tensor(count_le[:, :, :], count[:, :].unsqueeze(2).broadcast_to(wide),
                                   cc("steps").unsqueeze(1).broadcast_to(wide), ALU.is_gt))
            then(dve.tensor_reduce(tiles[:, :], count_le[:, :, :], AX.X, ALU.add))
            then(dve.tensor_tensor_scan(tiles_end[:, :], cc("ones")[:, 0:NX], tiles[:, :], 0.0, ALU.mult, ALU.add))
            wide = [P, NCH, NX]
            then(dve.tensor_tensor(past[:, :, :], tiles_end[:, :].unsqueeze(1).broadcast_to(wide),
                                   cc("tile").unsqueeze(2).broadcast_to(wide), ALU.is_le))
            then(dve.tensor_reduce(expert[:, :], past[:, :, :], AX.X, ALU.add))
            then(dve.tensor_tensor(past_tiles[:, :, :], past[:, :, :], tiles[:, :].unsqueeze(1).broadcast_to(wide),
                                   ALU.mult))
            then(dve.tensor_reduce(begun[:, :], past_tiles[:, :, :], AX.X, ALU.add))
            then(dve.tensor_scalar(live[:, :], expert[:, :], float(NX), float(P), ALU.is_lt, ALU.mult))
            then(dve.tensor_tensor(inside[:, :], cc("tile"), begun[:, :], ALU.subtract))
            then(dve.tensor_tensor(inside[:, :], inside[:, :], live[:, :], ALU.mult))
            then(dve.scalar_tensor_tensor(out=values[:, 0, :], in0=expert[:, :], scalar=float(REGION),
                                          in1=inside[:, :], op0=ALU.mult, op1=ALU.add))
            then(dve.tensor_scalar(values[:, 1, :], expert[:, :], float(NX - 1), None, ALU.min))
            dve.tensor_tensor(pad_f[:, :], count[:, :], cc("ebase"), ALU.add).then_inc(values_made, 1)
            dve.wait_ge(values_made, 1)
            dve.tensor_copy(pad_at[:, :], pad_f[0:1, :]).then_inc(tiles_known, 1)
            dve.wait_ge(values_turned, 1)
            dve.tensor_copy(tile_rows[:, :], bank(0)[0:1, 0:NCH * P]).then_inc(tiles_known, 1)
            dve.tensor_copy(tile_experts[:, 4:4 + NCH * P], bank(1)[0:1, 0:NCH * P]).then_inc(tiles_known, 1)
            dve.tensor_copy(expert_of[:, :], bank(1)[:, 0:NCH * P]).then_inc(tiles_known, 1)
            dve.wait_ge(tiles_known, 4)
            dve.tensor_copy(pad_f[0:1, 0:1], pad_f[0:1, 0:1]).then_inc(routed, 1)

            dve.wait_ge(routed, 2)
            for g in range(NGRP):
                dve.wait_ge(down_hi, g + 1)
                wide = slice(WG * E * g, WG * E * (g + 1))
                dve.tensor_tensor(w_dn[1][:, wide], w_dn[1][:, wide].bitcast(F32), w_dn[0][:, wide].bitcast(F32),
                                  ALU.subtract).then_inc(down_lo, 1)

            def frame_b(s):
                f, h = s.at(1), s.at(-1)
                if f.within(NS):
                    dve.wait_ge(rows_in[f.r], 32 * (f.q + 1))
                    if due(f.n - 1):
                        dve.wait_ge(weight_made, f.n - 1)
                    for i in range(2):
                        last = dve.scalar_tensor_tensor(
                            out=weights[f.r % 2][:, i, :], in0=cc("number"),
                            scalar=expert_of[:, bass.ds(f.n * 2 + i, 1)], in1=rows[f.r][:, i, E:E + NX],
                            op0=ALU.is_equal, op1=ALU.mult)
                    last.then_inc(weights_made, 1)
                    dve.tensor_copy(tokens[:, bass.ds(f.n * 2, 2)],
                                    rows[f.r][:, :, ROW - 1].bitcast(U32)).then_inc(tokens_made, 1)
                    dve.wait_ge(weights_made, f.n + 1)
                    if due(f.n - 1):
                        dve.wait_ge(inner_made, f.n - 1)
                    dve.tensor_reduce(weight[f.r % 2][:, :], weights[f.r % 2][:, :, :], AX.X,
                                      ALU.add).then_inc(weight_made, 1)
                    dve.wait_ge(x_hi, f.n + 1)
                    dve.tensor_tensor(x_t[1][f.r % 2][:, :, :, :].rearrange("p i c t -> p (i c t)"), x_t_p[f.r % 2],
                                      x_t[0][f.r % 2][:, :, :, :].rearrange("p i c t -> p (i c t)").bitcast(F32),
                                      ALU.subtract).then_inc(x_lo, 1)
                if s.within(NS):
                    dve.wait_ge(gated_made, s.n + 1)
                    dve.wait_ge(weight_made, s.n + 1)
                    if due(s.n - 1):
                        dve.wait_ge(h_turned, s.n - 1)
                    for i in range(2):
                        last = dve.scalar_tensor_tensor(
                            out=inner[s.r % 2][:, i, :], in0=gated[s.r % 2][:, i, :],
                            scalar=weight[s.r % 2][:, i:i + 1],
                            in1=gu_p[s.r % 2][:, 2 * I * i + I:2 * I * (i + 1)], op0=ALU.mult, op1=ALU.mult)
                    last.then_inc(inner_made, 1)
                if h.within(NS):
                    dve.wait_ge(h_hi, h.n + 1)
                    dve.tensor_tensor(h_t[1][h.r % 2][:, :, :].rearrange("i k t -> i (k t)"),
                                      h_t_p[h.r % 2][0:I, 0:2 * P],
                                      h_t[0][h.r % 2][:, :, :].rearrange("i k t -> i (k t)").bitcast(F32),
                                      ALU.subtract).then_inc(h_lo, 1)
                    for i in range(2):
                        if due(16 * (2 * h.q + h.r // 2 - 1)):
                            dve.wait_ge(added[(2 * h.r + i) % NACC], 16 * (2 * h.q + h.r // 2 - 1))
                    dve.wait_ge(tokens_made, h.n + 1)
                    settle(dve, turns)
                    dve.tensor_copy(targets[h.r][:, :],
                                    tokens[:, bass.ds(h.n * 2, 2)]).then_inc(targets_made, 1)
            run_frames(dve, frame_b, 4, -1, 4, NS - 12, NS, unroll=16)

            for n in range(T // P // CR):
                a = part[n % NPART]
                dve.wait_ge(part_in[n % NPART], 16 * NACC * (n // NPART + 1))
                dve.tensor_tensor(a[0][:, :], a[0][:, :], a[1][:, :], ALU.add).then_inc(half_sum[0], 1)
                dve.tensor_tensor(a[2][:, :], a[2][:, :], a[3][:, :], ALU.add).then_inc(half_sum[1], 1)
                if due(n + 1):
                    dve.wait_ge(half_sum[0], n + 1)
                if due(n + 1):
                    dve.wait_ge(half_sum[1], n + 1)
                dve.tensor_tensor(a[0][:, :], a[0][:, :], a[2][:, :], ALU.add).then_inc(summed, 1)

        @block.tensor
        def _(pe):
            turns = pe_turns
            pe.wait_ge(consts_in, 32)
            pe.wait_ge(consts_made, 11)

            def frame(s4):
                t = s4.pair
                after, front, chosen_t, placed_t = t.at(1), t.at(2), t.at(-2), t.at(-3)

                def scores(u, s):
                    pe.wait_ge(k_masked, s.n + 1)
                    pe.wait_ge(q_copied[u], s.n + 1)
                    if due(s.n):
                        pe.wait_ge(probs_made[u], s.n)
                    for n in range(4):
                        jp, gp = 2 * u + n // 2, n % 2
                        for b in range(2):
                            last = pe.matmul(scores_p[u][:, 2 * P * n:2 * P * (n + 1)],
                                             q_t[s.r][:, 2 * jp + gp, S * b:S * b + P],
                                             k_t[s.r][:, 2 * jp + b, :, :].rearrange("r g t -> r (g t)"),
                                             start=(b == 0), stop=(b == 1))
                    last.then_inc(scored[u], 1)

                def turn_sub(u):
                    pe.wait_ge(sub_made[u], t.n + 1)
                    flat = s_sub[u][:, :, :].rearrange("p x t -> p (x t)")
                    for n in range(8):
                        last = pe.transpose(scores_p[u][:, n * P:(n + 1) * P], flat[:, n * P:(n + 1) * P], ident)
                    last.then_inc(sub_turned[u], 1)

                def attend(u):
                    pe.wait_ge(probs_made[u], t.n + 1)
                    if u == 0:
                        pe.wait_ge(v_copied, t.n + 1)
                        if due(t.n):
                            pe.wait_ge(att_made, t.n)
                    for n in range(8):
                        jp, gp, jj = 2 * u + n // 4, (n // 2) % 2, n % 2
                        j = 4 * jj + jp
                        h = j * G + 2 * gp
                        for b in range(2):
                            last = pe.matmul(out_p[S * b:S * b + S, h:h + 2, :].rearrange("p h c -> p (h c)"),
                                             probs[u][:, n, S * b:S * b + S], v_t[t.r][:, b, j, :],
                                             start=True, stop=True)
                    last.then_inc(attended[u], 1)

                def turn_q(u):
                    if u == 0:
                        pe.wait_ge(q_lo, 2 * (front.n + 1))
                        if due(front.n):
                            pe.wait_ge(q_copied[0], front.n)
                    else:
                        pe.wait_ge(k_masked, front.n + 1)
                    for n in range(4):
                        last = pe.matmul(q_turn_p[u][:, n * P:(n + 1) * P],
                                         q_parts[:, 4 * u + n, :, :, :].rearrange("t jj p f -> t (jj p f)"),
                                         ident_r[:, :], start=True, stop=True)
                    last.then_inc(q_turned[u], 1)

                if placed_t.within(NT):
                    pe.wait_ge(mask_made, placed_t.n + 1)
                    pe.wait_ge(logits_copied, placed_t.n + 1)
                    pe.matmul(before_p, tri_b[:, :], mask[:, :], start=True, stop=True)
                    pe.matmul(tile_p, ones_b[:, :], mask[:, :], start=True, stop=True).then_inc(counted, 1)
                if t.within(NT):
                    turn_sub(0)
                    scores(1, t)
                if front.within(NT):
                    if due(front.n):
                        pe.wait_ge(q_copied[1], front.n)
                    pe.wait_ge(k_lo, 2 * (front.n + 1))
                    for n in range(4):
                        last = pe.matmul(k_turn_p[:, n * P:(n + 1) * P],
                                         k_parts[:, n, :, :, :].rearrange("t jj p w -> t (jj p w)"),
                                         ident_r[:, :], start=True, stop=True)
                    last.then_inc(k_turned, 1)
                if t.within(NT):
                    attend(0)
                if chosen_t.within(NT):
                    if due(chosen_t.n):
                        pe.wait_ge(base_moved, chosen_t.n)
                    pe.wait_ge(row_normed, chosen_t.n + 1)
                    for c in range(2):
                        last = pe.transpose(route_p[:, c * P:(c + 1) * P],
                                            row[s4.at(-2).r][:, c * P:(c + 1) * P], ident)
                    last.then_inc(x2_turned, 1)
                if after.within(NT):
                    scores(0, after)
                if chosen_t.within(NT):
                    pe.wait_ge(x2_copied, chosen_t.n + 1)
                    for c in range(2):
                        last = pe.matmul(logits_p, x2_t[:, c, :], gw[:, c, :], start=(c == 0), stop=(c == 1))
                    last.then_inc(logits_made, 1)
                if t.within(NT):
                    turn_sub(1)
                if front.within(NT):
                    turn_q(0)
                    turn_q(1)
                if t.within(NT):
                    attend(1)
            run_frames(pe, frame, 4, -2, 3, 27, NT + 2)

            pe.wait_ge(values_made, 1)
            for v in range(2):
                for c in range(NCH):
                    last = pe.matmul(bank(v)[:, c * P:(c + 1) * P], values[:, v, c:c + 1].broadcast_to([P, P]), ident,
                                     start=True, stop=True)
            last.then_inc(values_turned, 1)
            pe.wait_ge(values_turned, 1)
            pe.matmul(bank(2)[0:1, 0:1], values[:, 0, 0:1], ident[:, 0:1], start=True, stop=True).then_inc(routed, 1)
            pe.wait_ge(tiles_known, 4)
            expert_at = []

            def frame_b(s):
                f, h, b = s.at(1), s.at(-1), s.at(-2)
                if s.r == 0:
                    expert_at[:] = load_values(nc, mybir.EngineType.PE,
                                               tile_experts[0:1, bass.ds(s.q * 8, 12)], NX - 1)
                if f.within(NS):
                    pe.wait_ge(rows_in[f.r], 32 * (f.q + 1))
                    if due(f.n - 1):
                        pe.wait_ge(x_lo, f.n - 1)
                    for i in range(2):
                        for c in range(2):
                            last = pe.transpose(x_t_p[f.r % 2][:, (2 * i + c) * P:(2 * i + c + 1) * P],
                                                rows[f.r][:, i, c * P:(c + 1) * P], ident)
                    last.then_inc(x_turned, 1)
                if s.within(NS):
                    pe.wait_ge(x_lo, s.n + 1)
                    if due(s.n - 1):
                        pe.wait_ge(inner_made, s.n - 1)
                    settle(pe, turns)
                    for i in range(2):
                        at = expert_at[4 + 2 * s.r + i]
                        todo = [(c, xp, wp) for c in range(2) for xp, wp in ((0, 0), (0, 1), (1, 0))]
                        for n, (c, xp, wp) in enumerate(todo):
                            last = pe.matmul(gu_p[s.r % 2][:, 2 * I * i:2 * I * (i + 1)],
                                             x_t[xp][s.r % 2][:, i, c, :],
                                             w_gu[wp][:, c, bass.ds(at * (2 * I), 2 * I)],
                                             start=(n == 0), stop=(n == len(todo) - 1))
                    last.then_inc(gu_made, 1)
                if b.within(NS):
                    pe.wait_ge(h_lo, b.n + 1)
                    if due(b.n - 1):
                        pe.wait_ge(y_copied, b.n - 1)
                    pe.wait_ge(down_lo, NGRP)
                    settle(pe, turns)
                    for i in range(2):
                        at = expert_at[2 * s.r + i]
                        todo = ((0, 0), (0, 1), (1, 0))
                        for n, (hp, wp) in enumerate(todo):
                            last = pe.matmul(y_p[b.r % 2][:, i * E:(i + 1) * E], h_t[hp][b.r % 2][:, i, :],
                                             w_dn[wp][:, bass.ds(at * E, E)], start=(n == 0), stop=(n == 2))
                    last.then_inc(y_made, 1)
                if h.within(NS):
                    pe.wait_ge(inner_made, h.n + 1)
                    if due(h.n - 1):
                        pe.wait_ge(h_lo, h.n - 1)
                    for i in range(2):
                        last = pe.transpose(h_t_p[h.r % 2][0:I, i * P:(i + 1) * P], inner[h.r % 2][:, i, :], ident)
                    last.then_inc(h_turned, 1)
            run_frames(pe, frame_b, 4, -1, 4, NS - 12, NS + 1, unroll=16)


def kernel(x, ctx_512, L0_ffn_gate_w, L0_ffn_w_gate, L0_ffn_w_up, L0_ffn_w_down):
    import concourse.bacc as bacc
    from concourse.bass_utils import run_bass_kernel_spmd

    arrays = {"x": x, "ctx_in": ctx_512, "gate_w": L0_ffn_gate_w, "w_gate": L0_ffn_w_gate,
              "w_up": L0_ffn_w_up, "w_down": L0_ffn_w_down, "const": constants()}
    arrays = {name: np.ascontiguousarray(a) for name, a in arrays.items()}
    nc = bacc.Bacc("TRN2", target_bir_lowering=False, num_devices=1)
    ins = [nc.dram_tensor(name, a.shape, mybir.dt.from_np(a.dtype), kind="ExternalInput").ap()
           for name, a in arrays.items()]
    out = nc.dram_tensor("out", (B, S, E), F32, kind="ExternalOutput").ap()
    build(nc, *ins, out)
    r = run_bass_kernel_spmd(nc, [arrays], core_ids=[0])
    return r.results[0]["out"]
```
